# Optimizing a Trainium2 kernel written in Bass

```python
import numpy as np
import jax
import jax.numpy as jnp

def _softmax(x, axis=-1):
    return jax.nn.softmax(x, axis=axis)
def _gelu(x):
    return jax.nn.gelu(x, approximate=True)
def _silu(x):
    return jax.nn.silu(x)
def _sigmoid(x):
    return jax.nn.sigmoid(x)
def _layernorm(x, axis=-1, eps=1e-5):
    m = jnp.mean(x, axis=axis, keepdims=True)
    v = jnp.var(x, axis=axis, keepdims=True)
    return (x - m) / jnp.sqrt(v + eps)
def _scatter_add(tgt, idx, src, axis=0):
    return tgt.at[idx].add(src)
def _segment_sum(src, seg, n):
    return jax.ops.segment_sum(src, seg, n)

kernel_name = 'mk_conv_preact_d1_conv_nchw256_3f8388'

def setup_inputs(seed: int = 0):
    np.random.seed(seed)
    _w = jnp.asarray
    def _rec_inputs():
        import jax
        import jax.numpy as jnp
        _gk = jax.random.key(seed)
        x = 7.22e-05 + 1 * jax.random.normal(jax.random.fold_in(_gk, 1), (8, 256, 64, 64), jnp.float32)
        return x
    x = _rec_inputs()
    def _L0_conv_setup():
        import jax, jax.numpy as jnp
        import numpy as np
        K = 3

        def _extract_patches(x):
            b, n, h, w = x.shape
            xp = jnp.pad(x, ((0, 0), (0, 0), (1, 1), (1, 1)))
            slices = [xp[:, :, i:i + h, j:j + w] for i in range(K) for j in range(K)]
            return jnp.stack(slices, axis=2)

        def _conv3x3(x, w, b):
            y = jax.lax.conv_general_dilated(x, w, window_strides=(1, 1), padding=((1, 1), (1, 1)), dimension_numbers=('NCHW', 'OIHW', 'NCHW'))
            return y + b[None, :, None, None]
        key = jax.random.key(seed)
        ks = jax.random.split(key, 6)
        b, n, h, w = (8, 256, 64, 64)
        cout, r = (256, 4)
        cm = n // r
        s = lambda fan: 1.0 / np.sqrt(fan)
        return {'x': jax.random.normal(ks[0], (b, n, h, w), jnp.float32), 'w_c1': jax.random.normal(ks[1], (cm, n), jnp.float32) * s(n), 'b_c1': jnp.zeros((cm,), jnp.float32), 'w_c2': jax.random.normal(ks[2], (n, cm), jnp.float32) * s(cm), 'b_c2': jnp.zeros((n,), jnp.float32), 'w_d1': jax.random.normal(ks[3], (cm, n, 3, 3), jnp.float32) * s(n * 9), 'b_d1': jnp.zeros((cm,), jnp.float32), 'w_d2': jax.random.normal(ks[4], (K * K, cm), jnp.float32) * s(cm), 'b_d2': jnp.zeros((K * K,), jnp.float32), 'W': jax.random.normal(ks[5], (cout, n, K * K), jnp.float32) * s(n * K * K)}
    _L0_conv_all = _L0_conv_setup()
    _L0_conv_in = {k: v for k, v in _L0_conv_all.items() if k in ('w_c1', 'b_c1', 'w_c2', 'b_c2', 'w_d1', 'b_d1', 'w_d2', 'b_d2', 'W', )}
    del _L0_conv_all

    return {
        "x": x,
        "L0_conv_w_c1": _L0_conv_in["w_c1"],
        "L0_conv_b_c1": _L0_conv_in["b_c1"],
        "L0_conv_w_c2": _L0_conv_in["w_c2"],
        "L0_conv_b_c2": _L0_conv_in["b_c2"],
        "L0_conv_w_d1": _L0_conv_in["w_d1"],
        "L0_conv_b_d1": _L0_conv_in["b_d1"],
        "L0_conv_w_d2": _L0_conv_in["w_d2"],
        "L0_conv_b_d2": _L0_conv_in["b_d2"],
        "L0_conv_W": _L0_conv_in["W"],
    }

def reference(x, L0_conv_w_c1, L0_conv_b_c1, L0_conv_w_c2, L0_conv_b_c2, L0_conv_w_d1, L0_conv_b_d1, L0_conv_w_d2, L0_conv_b_d2, L0_conv_W):
    import jax
    import jax.numpy as jnp
    def _L0_conv_ref(x, w_c1, b_c1, w_c2, b_c2, w_d1, b_d1, w_d2, b_d2, W):
        import jax, jax.numpy as jnp
        import numpy as np
        K = 3

        def _extract_patches(x):
            b, n, h, w = x.shape
            xp = jnp.pad(x, ((0, 0), (0, 0), (1, 1), (1, 1)))
            slices = [xp[:, :, i:i + h, j:j + w] for i in range(K) for j in range(K)]
            return jnp.stack(slices, axis=2)

        def _conv3x3(x, w, b):
            y = jax.lax.conv_general_dilated(x, w, window_strides=(1, 1), padding=((1, 1), (1, 1)), dimension_numbers=('NCHW', 'OIHW', 'NCHW'))
            return y + b[None, :, None, None]
        yc = jax.nn.relu(jnp.einsum('bnhw,mn->bmhw', x, w_c1) + b_c1[None, :, None, None])
        c = jnp.einsum('bmhw,nm->bnhw', yc, w_c2) + b_c2[None, :, None, None]
        yd = jax.nn.relu(_conv3x3(x, w_d1, b_d1))
        d = jnp.einsum('bmhw,km->bkhw', yd, w_d2) + b_d2[None, :, None, None]
        patches = _extract_patches(x)
        attn = 1.0 + jnp.tanh(d[:, None, :, :, :] + c[:, :, None, :, :])
        out = jnp.einsum('bnkhw,onk->bohw', patches * attn, W)
        return out

    def _gn(v, G=32, eps=1e-5):
        B_, C_, H_, W_ = v.shape
        g = v.reshape(B_, G, C_ // G, H_, W_)
        m = jnp.mean(g, axis=(2, 3, 4), keepdims=True)
        s = jnp.var(g, axis=(2, 3, 4), keepdims=True)
        return ((g - m) / jnp.sqrt(s + eps)).reshape(v.shape)

    def _ln_c(v, eps=1e-6):
        m = jnp.mean(v, axis=1, keepdims=True)
        s = jnp.var(v, axis=1, keepdims=True)
        return (v - m) / jnp.sqrt(s + eps)

    def _ln_t(v, eps=1e-5):
        m = jnp.mean(v, axis=-1, keepdims=True)
        s = jnp.var(v, axis=-1, keepdims=True)
        return (v - m) / jnp.sqrt(s + eps)

    def _to_tokens(v):
        B_, C_, H_, W_ = v.shape
        return v.reshape(B_, C_, H_ * W_).transpose(0, 2, 1)
    def _from_tokens(t, like):
        B_, C_, H_, W_ = like.shape
        return t.transpose(0, 2, 1).reshape(B_, C_, H_, W_)

    x = x + _L0_conv_ref(_gn(x), L0_conv_w_c1, L0_conv_b_c1, L0_conv_w_c2, L0_conv_b_c2, L0_conv_w_d1, L0_conv_b_d1, L0_conv_w_d2, L0_conv_b_d2, L0_conv_W)
    return x


_drawn_inputs = setup_inputs


def setup_inputs(seed=0):
    import zlib

    import numpy as np

    out = dict(_drawn_inputs(seed))
    spreads = {'L0_conv_b_c1': (0.0, 0.1),
     'L0_conv_b_c2': (0.0, 0.1),
     'L0_conv_b_d1': (0.0, 0.302),
     'L0_conv_b_d2': (0.0, 0.1)}
    factors = {}
    for name, (base, spread) in spreads.items():
        noise = np.random.default_rng([zlib.crc32(name.encode()), seed]).standard_normal(out[name].shape)
        drawn = base * np.exp(spread * noise) if base else spread * noise
        out[name] = jnp.asarray(drawn.astype(out[name].dtype))
    for name, factor in factors.items():
        out[name] = (out[name] * factor).astype(out[name].dtype)
    return out
```

```python
from contextlib import ExitStack

import concourse.bass as bass
from concourse import mybir

F32 = mybir.dt.float32
F16 = mybir.dt.float16
BF16 = mybir.dt.bfloat16
I32 = mybir.dt.int32
ALU = mybir.AluOpType
ACT = mybir.ActivationFunctionType
AX = mybir.AxisListType

P = 128
TAPS = 9
GROUP = 8
X_SCALE = 128.0
W_TOP = 2.0 ** 14
W_TINY = 1e-30
EPS = 1e-5
D_ROWS = 73
LEAD = 4
ROLL = 5
DRAIN_AT = 4
STATS_AT = 5
CONV_SLOTS = 7


def build(nc, x, w_d1, w_c1, w_out, w_s0, w_d2, vecs, delta, group_avg, out):
    B, C, R, COLS = x.shape
    H = C // P
    M = w_d1.shape[-1]
    BR = 512 // COLS
    N = BR * COLS
    PAIRS = R // (2 * BR)
    PR = 2 * BR
    SR, SC = PR + 2, COLS + 2
    STEPS = 2 * TAPS
    IMG = PAIRS * STEPS
    CHUNKS = H * R * COLS // 512
    assert H == 2 and M == 64 and N == 512 and IMG % 4 == 0 and PAIRS == 4

    x_v = x.rearrange("b (h p) (q r) c -> b q p h (r c)", p=P, q=PAIRS)
    out_v = out.rearrange("b (h p) (q r) c -> b q p h (r c)", p=P, q=PAIRS)

    with ExitStack() as ctx:
        def sb(name, shape, dt=F32):
            return ctx.enter_context(nc.sbuf_tensor(name, shape, dt))

        def ps(name, shape):
            return ctx.enter_context(nc.psum_tensor(name, shape, F32))

        def sem(name):
            return ctx.enter_context(nc.semaphore(name))

        xraw = sb("xraw", [P, 2, H, R * COLS])
        xn = sb("xn", [P, PAIRS, H, SR, SC])
        xh = sb("xh", [P, 2, H, SR, SC], F16)
        xl = sb("xl", [P, 2, H, SR, SC], F16)
        wh = sb("wh", [P, H, TAPS, C], F16)
        wl = sb("wl", [P, H, TAPS, C], F16)
        wdh = sb("wdh", [P, H, TAPS, M], F16)
        wdl = sb("wdl", [P, H, TAPS, M], F16)
        wch = sb("wch", [P, H, M], F16)
        wcl = sb("wcl", [P, H, M], F16)
        ws0 = sb("ws0", [P, 2, C])
        wd2 = sb("wd2", [P, 2, D_ROWS])
        dsel16 = sb("dsel16", [D_ROWS, TAPS - 1, P], F16)
        dsel = sb("dsel", [D_ROWS, TAPS - 1, P], BF16)
        gavg = sb("gavg", [P, P])
        vec = sb("vec", [P, 6])
        tbias = sb("tbias", [P, H])
        wmax = sb("wmax", [P, 3])
        wmaxall = sb("wmaxall", [P, 3])
        wexp = sb("wexp", [P, 3])
        wtmp = sb("wtmp", [P, 3])
        wscale = sb("wscale", [P, 3])
        wdescale = sb("wdescale", [P, 3])
        yscale = sb("yscale", [P, 2])
        bnst = sb("bnst", [P, H, CHUNKS // H, 6])
        chan = sb("chan", [P, H, 2])
        gmean = sb("gmean", [P, H])
        gdev = sb("gdev", [P, H])
        gdev2 = sb("gdev2", [P, H])
        gsq = sb("gsq", [P, H])
        gvar = sb("gvar", [P, H])
        ghalf = sb("ghalf", [P, H])
        grs = sb("grs", [P, H])
        gn1 = sb("gn1", [P, H])
        gn2 = sb("gn2", [P, H])
        gn3 = sb("gn3", [P, H])
        rstd = sb("rstd", [P, H])
        y = sb("y", [P, 2, N])
        dsb = sb("dsb", [D_ROWS, 2, N])
        dres = sb("dres", [D_ROWS, 2, N])
        dpart = sb("dpart", [D_ROWS, 2, 2, N], BF16)
        t = sb("t", [P, 2, H, N])
        u = sb("u", [P, 2, H, N])
        uh = sb("uh", [P, 4, H, N], F16)
        ul = sb("ul", [P, 4, H, N], F16)
        osb = sb("osb", [P, H, 2 * N])

        acc = ps("acc", [P, 2, 2, N])
        sc = ps("sc", [P, H, N])
        yp = ps("yp", [P, 2, N])

        spare = xraw[:, 1, :, :].rearrange("p h n -> p (h n)")
        nW, nD, nC = H * TAPS * C, H * TAPS * M, H * M
        wf = [spare[:, 0:nD], spare[:, nD:nD + nC], spare[:, nD + nC:nD + nC + nW]]
        w_hi = [wdh[:].rearrange("p h k m -> p (h k m)"), wch[:].rearrange("p h m -> p (h m)"),
                wh[:].rearrange("p h k m -> p (h k m)")]
        w_lo = [wdl[:].rearrange("p h k m -> p (h k m)"), wcl[:].rearrange("p h m -> p (h m)"),
                wl[:].rearrange("p h k m -> p (h k m)")]

        x_loaded = [sem(f"x_loaded{q}") for q in range(PAIRS)]
        w_loaded = [sem(f"w_loaded{n}") for n in range(3)]
        c_loaded = sem("c_loaded")
        zeroed = sem("zeroed")
        wmax_done = sem("wmax_done")
        wred_done = sem("wred_done")
        wscale_done = sem("wscale_done")
        whi_done = sem("whi_done")
        wlo_done = sem("wlo_done")
        const_done = sem("const_done")
        chain = sem("chain")
        bn_done = sem("bn_done")
        chan_done = sem("chan_done")
        gmean_done = sem("gmean_done")
        gcopy_done = sem("gcopy_done")
        gdev_done = sem("gdev_done")
        gsq_done = sem("gsq_done")
        gvar_done = sem("gvar_done")
        geps_done = sem("geps_done")
        gpow_done = sem("gpow_done")
        gnewton = sem("gnewton")
        xn_done = sem("xn_done")
        xh_done = sem("xh_done")
        xl_done = sem("xl_done")
        conv_done = sem("conv_done")
        y_done = sem("y_done")
        d_done = sem("d_done")
        dsb_done = sem("dsb_done")
        dstep = sem("dstep")
        dpart_done = sem("dpart_done")
        s_done = sem("s_done")
        t_done = sem("t_done")
        u_done = sem("u_done")
        hi_done = sem("hi_done")
        lo_done = sem("lo_done")
        used = sem("used")
        drained = sem("drained")
        stored = sem("stored")

        U0, HI0, LO0, USED0, DR0, ST0 = 4, 2, 2, 4, 4, 16

        block = ctx.enter_context(nc.Block())

        def pairs_of(q):
            return (1 if q == 0 else 0), (SR - 1 if q == PAIRS - 1 else SR)

        @block.sync
        def _(sp):
            sp.sem_inc(stored, ST0)
            sp.dma_start(wf[0], w_d1.rearrange("p h k m -> p (h k m)")).then_inc(w_loaded[0], 16)
            sp.dma_start(wf[1], w_c1.rearrange("p h m -> p (h m)")).then_inc(w_loaded[1], 16)
            for q in range(PAIRS):
                sp.dma_start(xraw[:, 0, :, q * PR * COLS:(q + 1) * PR * COLS], x_v[0, q]).then_inc(x_loaded[q], 16)
            sp.dma_start(wf[2], w_out.rearrange("p h k m -> p (h k m)")).then_inc(w_loaded[2], 16)
            sp.wait_ge(wlo_done, 3)
            for q in range(PAIRS):
                sp.dma_start(xraw[:, 1, :, q * PR * COLS:(q + 1) * PR * COLS], x_v[1, q]).then_inc(x_loaded[q], 16)

            def image(i, load):
                for q in range(PAIRS):
                    sp.wait_ge(drained, 4 * (PAIRS * i + q) + 4 + DR0)
                    sp.dma_start(out_v[i, q], osb[:]).then_inc(stored, 16)
                    if load:
                        sp.dma_start(xraw[:, i % 2, :, q * PR * COLS:(q + 1) * PR * COLS],
                                     x_v[i + 2, q]).then_inc(x_loaded[q], 16)

            with sp.Fori(0, B - 2) as i:
                image(i, True)
            image(B - 2, False)
            image(B - 1, False)
            sp.wait_ge(stored, 16 * B * PAIRS + ST0)

        @block.gpsimd
        def _(pool):
            nc.gpsimd.memset(ghalf[:], -0.5)
            nc.gpsimd.memset(xn[:], 0.0).then_inc(zeroed, 1)

            def tensor_max(n):
                pool.wait_ge(wmax_done, n + 1)
                nc.gpsimd.partition_all_reduce(wmaxall[:, n:n + 1], wmax[:, n:n + 1], P,
                                               bass.bass_isa.ReduceOp.max).then_inc(wred_done, 1)

            def root(image):
                pool.wait_ge(geps_done, image + 1)
                nc.gpsimd.tensor_tensor(grs[:], gvar[:], ghalf[:], ALU.pow).then_inc(gpow_done, 1)

            tensor_max(0)
            tensor_max(1)
            root(0)
            tensor_max(2)
            with pool.Fori(1, B) as i:
                root(i)

        @block.scalar
        def _(act):
            act.dma_start(vec[:], vecs).then_inc(c_loaded, 16)
            act.dma_start(gavg[:], group_avg).then_inc(c_loaded, 16)
            act.dma_start(ws0[:], w_s0).then_inc(c_loaded, 16)
            act.dma_start(wd2[:], w_d2).then_inc(c_loaded, 16)
            act.dma_start(dsel16[:], delta).then_inc(c_loaded, 16)

            def weights_high(n):
                act.wait_ge(w_loaded[n], 16)
                act.wait_ge(wscale_done, n + 1)
                nc.scalar.activation(w_hi[n], wf[n], ACT.Copy, scale=wscale[:, n:n + 1]).then_inc(whi_done, 1)

            def tanh(g, l):
                for h in range(H):
                    act.wait_ge(s_done, 2 * g + h + 1)
                    act.wait_ge(u_done, 2 * (g - 2) + h + 1 + U0)
                    nc.scalar.activation(t[:, l % 2, h, :], sc[:, h, :], ACT.Tanh,
                                         bias=tbias[:, h:h + 1]).then_inc(t_done, 1)

            def high(g, l):
                act.wait_ge(u_done, 2 * g + 2 + U0)
                act.wait_ge(used, g - 3 + USED0)
                nc.scalar.activation(uh[:, l % 4, :, :], u[:, l % 2, :, :], ACT.Copy).then_inc(hi_done, 1)

            def x_high(p, q):
                act.wait_ge(xn_done, p + 1)
                nc.scalar.activation(xh[:, q % 2].rearrange("p h r c -> p (h r c)"),
                                     xn[:, q].rearrange("p h r c -> p (h r c)"), ACT.Copy).then_inc(xh_done, 1)

            def hidden(p):
                act.wait_ge(conv_done, p + 1)
                for b in range(2):
                    ins = nc.scalar.activation(y[:, b, :], yp[:, b, :], ACT.Relu,
                                               bias=vec[:, b:b + 1], scale=yscale[:, b:b + 1])
                ins.then_inc(y_done, 1)

            def tap_bias(p):
                act.wait_ge(d_done, p + 1)
                nc.scalar.activation(dsb[:], yp[0:D_ROWS, :, :], ACT.Identity,
                                     bias=vec[0:D_ROWS, 4:5]).then_inc(dsb_done, 1)

            act.wait_ge(c_loaded, 5 * 16)
            act.wait_ge(zeroed, 1)
            weights_high(0)
            weights_high(1)
            x_high(0, 0)
            act.wait_ge(const_done, 1)
            x_high(1, 1)
            weights_high(2)
            hidden(0)
            tap_bias(0)

            def step(i, l, last):
                q, e = divmod(l, STEPS)
                g, p = IMG * i + l, PAIRS * i + q
                tanh(g, l)
                if not (isinstance(g, int) and g == 0):
                    high(g - 1, (l - 1) % IMG)
                if e == 3 and not (last and q >= PAIRS - 2):
                    x_high(p + 2, (q + 2) % PAIRS)
                if e == 13 and not (last and q == PAIRS - 1):
                    hidden(p + 1)
                if e == 14 and not (last and q == PAIRS - 1):
                    tap_bias(p + 1)

            for l in range(ROLL):
                step(0, l, False)
            with act.Fori(0, B - 1) as i:
                for l in range(ROLL, IMG):
                    step(i, l, False)
                for l in range(ROLL):
                    step(i + 1, l, False)
            for l in range(ROLL, IMG):
                step(B - 1, l, True)
            high(B * IMG - 1, IMG - 1)

        @block.vector
        def _(dve):
            for s, n in ((u_done, U0), (hi_done, HI0), (lo_done, LO0), (drained, DR0)):
                dve.sem_inc(s, n)
            links = [0]

            def link(ins):
                links[0] += 1
                ins.then_inc(chain, 1)
                dve.wait_ge(chain, links[0])

            def weight_scale(n):
                dve.wait_ge(w_loaded[n], 16)
                nc.vector.tensor_reduce(wmax[:, n:n + 1], wf[n], AX.X, ALU.max,
                                        apply_absolute_value=True).then_inc(wmax_done, 1)

            def weight_scale_2(n):
                dve.wait_ge(wred_done, n + 1)
                c = slice(n, n + 1)
                link(nc.vector.tensor_scalar(wtmp[:, c], wmaxall[:, c], W_TINY, None, ALU.max))
                link(nc.vector.tensor_scalar(wexp[:, c].bitcast(I32), wtmp[:, c].bitcast(I32), 0x7F800000, None,
                                             ALU.bitwise_and))
                link(nc.vector.tensor_scalar(wtmp[:, c], wexp[:, c], 1.0 / W_TOP, None, ALU.mult))
                link(nc.vector.tensor_scalar(wdescale[:, c], wexp[:, c], 1.0 / (W_TOP * X_SCALE), None, ALU.mult))
                nc.vector.reciprocal(wscale[:, c], wtmp[:, c]).then_inc(wscale_done, 1)

            def weights_low(n):
                dve.wait_ge(whi_done, n + 1)
                dve.wait_ge(wscale_done, n + 1)
                nc.vector.scalar_tensor_tensor(out=w_lo[n], in0=wf[n], scalar=wscale[:, n:n + 1], in1=w_hi[n],
                                               op0=ALU.mult, op1=ALU.subtract).then_inc(wlo_done, 1)

            def stats(image, par, c):
                q, r = divmod(c, CHUNKS // PAIRS)
                h, k = divmod(r, CHUNKS // PAIRS // H)
                n = q * (CHUNKS // PAIRS // H) + k
                if r == 0:
                    dve.wait_ge(x_loaded[q], 16 * image + 16)
                ins = nc.vector.bn_stats(bnst[:, h, n, :], xraw[:, par, h, 512 * n:512 * n + 512])
                if c == CHUNKS - 1:
                    ins.then_inc(bn_done, 1)

            def chan_stats(image):
                for h in range(H):
                    ins = nc.vector.bn_aggr(chan[:, h, :], bnst[:, h].rearrange("p n s -> p (n s)"))
                ins.then_inc(chan_done, 1)

            def group_dev(image):
                dve.wait_ge(gmean_done, image + 1)
                nc.vector.tensor_copy(gmean[:], acc[:, 1, 0, 0:H]).then_inc(gcopy_done, 1)
                dve.wait_ge(gcopy_done, image + 1)
                nc.vector.tensor_tensor(gdev[:], chan[:, :, 0], gmean[:], ALU.subtract).then_inc(gdev_done, 1)
                dve.wait_ge(gdev_done, 2 * image + 1)
                nc.vector.tensor_tensor(gdev2[:], gdev[:], gdev[:], ALU.mult).then_inc(gdev_done, 1)
                dve.wait_ge(gdev_done, 2 * image + 2)
                nc.vector.tensor_tensor(gsq[:], gdev2[:], chan[:, :, 1], ALU.add).then_inc(gsq_done, 1)

            def group_eps(image):
                dve.wait_ge(gvar_done, image + 1)
                nc.vector.tensor_scalar(gvar[:], acc[:, 1, 0, 0:H], EPS, None, ALU.add).then_inc(geps_done, 1)

            def group_root(image):
                dve.wait_ge(gpow_done, image + 1)
                nc.vector.tensor_tensor(gn1[:], grs[:], grs[:], ALU.mult).then_inc(gnewton, 1)
                dve.wait_ge(gnewton, 4 * image + 1)
                nc.vector.tensor_tensor(gn2[:], gn1[:], gvar[:], ALU.mult).then_inc(gnewton, 1)
                dve.wait_ge(gnewton, 4 * image + 2)
                nc.vector.tensor_scalar(gn3[:], gn2[:], -0.5 * X_SCALE, 1.5 * X_SCALE, ALU.mult,
                                        ALU.add).then_inc(gnewton, 1)
                dve.wait_ge(gnewton, 4 * image + 3)
                nc.vector.tensor_tensor(rstd[:], grs[:], gn3[:], ALU.mult).then_inc(gnewton, 1)

            def normalise(image, par, p, q):
                dve.wait_ge(gnewton, 4 * image + 4)
                r0, r1 = pairs_of(q)
                for h in range(H):
                    src = xraw[:, par, h, (q * PR - 1 + r0) * COLS:(q * PR - 1 + r1) * COLS]
                    ins = nc.vector.tensor_scalar(xn[:, q, h, r0:r1, 1:1 + COLS],
                                                  src.rearrange("p (r c) -> p r c", c=COLS),
                                                  gmean[:, h:h + 1], rstd[:, h:h + 1], ALU.subtract, ALU.mult)
                ins.then_inc(xn_done, 1)

            def x_low(p, q):
                dve.wait_ge(xh_done, p + 1)
                nc.vector.tensor_tensor(xl[:, q % 2].rearrange("p h r c -> p (h r c)"),
                                        xn[:, q].rearrange("p h r c -> p (h r c)"),
                                        xh[:, q % 2].rearrange("p h r c -> p (h r c)"),
                                        ALU.subtract).then_inc(xl_done, 1)

            def split_taps(p, q):
                d = dpart[:, q % 2]
                dve.wait_ge(dsb_done, p + 1)
                nc.vector.tensor_copy(d, dsb[:]).then_inc(dstep, 1)
                dve.wait_ge(dstep, 3 * p + 1)
                nc.vector.tensor_tensor(dres[:], dsb[:], d, ALU.subtract).then_inc(dstep, 1)

            def split_taps_2(p, q):
                d = dpart[:, q % 2]
                dve.wait_ge(dstep, 3 * p + 2)
                nc.vector.tensor_copy(d[0:32 + TAPS], dres[0:32 + TAPS]).then_inc(dstep, 1)
                dve.wait_ge(dstep, 3 * p + 3)
                nc.vector.tensor_tensor(d[0:TAPS], dres[0:TAPS], d[0:TAPS], ALU.subtract).then_inc(dpart_done, 1)

            def gate(g, l):
                q, e = divmod(l, STEPS)
                b, k = divmod(e, TAPS)
                dy, dx = divmod(k, 3)
                dve.wait_ge(hi_done, g - 1 + HI0)
                dve.wait_ge(lo_done, g - 1 + LO0)
                for h in range(H):
                    dve.wait_ge(t_done, 2 * g + h + 1)
                    nc.vector.scalar_tensor_tensor(
                        out=u[:, l % 2, h, :].rearrange("p (r c) -> p r c", c=COLS),
                        in0=t[:, l % 2, h, :].rearrange("p (r c) -> p r c", c=COLS), scalar=1.0,
                        in1=xn[:, q, h, b * BR + dy:b * BR + dy + BR, dx:dx + COLS],
                        op0=ALU.add, op1=ALU.mult).then_inc(u_done, 1)

            def low(g, l):
                dve.wait_ge(hi_done, g + 1 + HI0)
                nc.vector.tensor_tensor(ul[:, l % 4, :, :], u[:, l % 2, :, :], uh[:, l % 4, :, :],
                                        ALU.subtract).then_inc(lo_done, 1)

            def drain(par, n, q, b):
                dve.wait_ge(used, TAPS * (n + 1) + USED0)
                if b == 0:
                    dve.wait_ge(stored, 8 * n + ST0)
                for m in range(H):
                    a = (q * PR + b * BR) * COLS
                    nc.vector.scalar_tensor_tensor(out=osb[:, m, b * N:(b + 1) * N], in0=acc[:, b, m, :],
                                                   scalar=wdescale[:, 2:3], in1=xraw[:, par, m, a:a + N],
                                                   op0=ALU.mult, op1=ALU.add).then_inc(drained, 1)

            weight_scale(0)
            weight_scale(1)
            weight_scale_2(0)
            weight_scale_2(1)
            dve.wait_ge(c_loaded, 5 * 16)
            for b in range(2):
                for half, n in ((b, 0), (1 - b, 1)):
                    rows = slice(M * half, M * half + M)
                    nc.vector.tensor_copy(yscale[rows, b:b + 1], wdescale[rows, n:n + 1])
            for h in range(H):
                nc.vector.tensor_tensor(tbias[:, h:h + 1], vec[:, 2 + h:3 + h], vec[:, 5:6], ALU.add)
            nc.vector.tensor_copy(dsel[:], dsel16[:]).then_inc(const_done, 1)
            weights_low(0)
            weights_low(1)
            for c in range(CHUNKS):
                stats(0, 0, c)
            dve.wait_ge(bn_done, 1)
            chan_stats(0)
            group_dev(0)
            group_eps(0)
            group_root(0)
            dve.wait_ge(zeroed, 1)
            normalise(0, 0, 0, 0)
            x_low(0, 0)
            normalise(0, 0, 1, 1)
            weight_scale(2)
            weight_scale_2(2)
            x_low(1, 1)
            weights_low(2)
            split_taps(0, 0)
            split_taps_2(0, 0)

            def step(i, l, last):
                q, e = divmod(l, STEPS)
                g, p = IMG * i + l, PAIRS * i + q
                if e == 0:
                    dve.wait_ge(xn_done, p + 1)
                if l == STATS_AT + CHUNKS and not last:
                    dve.wait_ge(bn_done, i + 2)
                gate(g, l)
                if not (isinstance(g, int) and g == 0):
                    low(g - 1, (l - 1) % IMG)
                if e == 1 and not (last and q >= PAIRS - 2):
                    if q < PAIRS - 2:
                        normalise(i, i % 2, p + 2, q + 2)
                    else:
                        normalise(i + 1, (i + 1) % 2, p + 2, q + 2 - PAIRS)
                if e == DRAIN_AT and q > 0:
                    drain(i % 2, 2 * p - 1, q - 1, 1)
                if l == DRAIN_AT and not (isinstance(i, int) and i == 0):
                    drain((i + 1) % 2, 2 * p - 1, PAIRS - 1, 1)
                if e == 5 and not (last and q >= PAIRS - 2):
                    x_low(p + 2, (q + 2) % PAIRS)
                if e == TAPS + DRAIN_AT:
                    drain(i % 2, 2 * p, q, 0)
                if e == 15 and not (last and q == PAIRS - 1):
                    split_taps(p + 1, q + 1)
                if e == 16 and not (last and q == PAIRS - 1):
                    split_taps_2(p + 1, q + 1)
                if not last:
                    if STATS_AT <= l < STATS_AT + CHUNKS:
                        stats(i + 1, (i + 1) % 2, l - STATS_AT)
                    if l == STATS_AT + CHUNKS:
                        chan_stats(i + 1)
                    if q == 1 and e == 8:
                        group_dev(i + 1)
                    if q == 1 and e == 11:
                        group_eps(i + 1)
                    if q == 1 and e == 13:
                        group_root(i + 1)

            for l in range(ROLL):
                step(0, l, False)
            with dve.Fori(0, B - 1) as i:
                for l in range(ROLL, IMG):
                    step(i, l, False)
                for l in range(ROLL):
                    step(i + 1, l, False)
            for l in range(ROLL, IMG):
                step(B - 1, l, True)
            low(B * IMG - 1, IMG - 1)
            drain((B - 1) % 2, 2 * PAIRS * B - 1, PAIRS - 1, 1)

        @block.tensor
        def _(pe):
            pe.sem_inc(used, USED0)

            def scores(g, l, p):
                q, e = divmod(l, STEPS)
                b, k = divmod(e, TAPS)
                if k == 0 and b == 0:
                    pe.wait_ge(y_done, p + 1)
                if k == 1 and b == 0:
                    pe.wait_ge(dpart_done, p + 1)
                for h in range(H):
                    if not (isinstance(g, int) and g == 0):
                        pe.wait_ge(t_done, 2 * (g - 1) + h + 1)
                    if k == 0:
                        ins = nc.tensor.matmul(sc[:, h, :], ws0[:, b, h * P:(h + 1) * P], y[:, b, :],
                                               start=True, stop=True)
                    else:
                        ins = nc.tensor.matmul(sc[:, h, :], dsel[:, k - 1, :], dpart[:, q % 2, b, :],
                                               start=False, stop=True, skip_group_check=True)
                    ins.then_inc(s_done, 1)

            def outputs(g, l, n):
                b, k = divmod(l % STEPS, TAPS)
                pe.wait_ge(lo_done, g + 1 + LO0)
                if k == 0:
                    pe.wait_ge(drained, 2 * (n - 1) + DR0)
                for h in range(H):
                    for m in range(H):
                        cols = slice(m * P, (m + 1) * P)
                        for j, (w, v) in enumerate(((wh, uh), (wh, ul), (wl, uh))):
                            ins = nc.tensor.matmul(acc[:, b, m, :], w[:, h, k, cols], v[:, l % 4, h, :],
                                                   start=(k == 0 and h == 0 and j == 0),
                                                   stop=(k == TAPS - 1 and h == H - 1 and j == 2))
                ins.then_inc(used, 1)

            slots = [(0, h, k, j) for h in range(H) for k in range(TAPS) for j in range(3)]
            slots += [(1, h, TAPS // 2, j) for h in range(H) for j in range(3)]

            def hidden_slots(q, first, count, signal=True):
                for s in range(first, min(first + count, len(slots))):
                    kind, h, k, j = slots[s]
                    dy, dx = divmod(k, 3)
                    x_part = (xh, xl, xh)[j]
                    for b in range(2):
                        half = b if kind == 0 else 1 - b
                        w = ((wdh, wdh, wdl)[j][:, h, k, :], (wch, wch, wcl)[j][:, h, :])[kind]
                        ins = nc.tensor.matmul(
                            yp[M * half:M * half + M, b, :], w,
                            x_part[:, q % 2, h, b * BR + dy:b * BR + dy + BR, dx:dx + COLS],
                            start=(h == 0 and j == 0 and (kind == 1 or k == 0)),
                            stop=(h == H - 1 and j == 2 and (kind == 1 or k == TAPS - 1)))
                    if s == len(slots) - 1:
                        ins.then_inc(conv_done, 1)

            def tap_products(p):
                pe.wait_ge(y_done, p + 1)
                for b in range(2):
                    ins = nc.tensor.matmul(yp[0:D_ROWS, b, :], wd2[:, b, :], y[:, b, :], start=True, stop=True)
                ins.then_inc(d_done, 1)

            def group_mean(image):
                pe.wait_ge(chan_done, image + 1)
                nc.tensor.matmul(acc[:, 1, 0, 0:H], gavg[:], chan[:, :, 0], start=True,
                                 stop=True).then_inc(gmean_done, 1)

            def group_var(image):
                pe.wait_ge(gsq_done, image + 1)
                nc.tensor.matmul(acc[:, 1, 0, 0:H], gavg[:], gsq[:], start=True, stop=True).then_inc(gvar_done, 1)

            pe.wait_ge(c_loaded, 5 * 16)
            group_mean(0)
            group_var(0)
            pe.wait_ge(wlo_done, 2)
            pe.wait_ge(xl_done, 1)
            hidden_slots(0, 0, len(slots))
            tap_products(0)
            pe.wait_ge(const_done, 1)
            for g in range(LEAD):
                scores(g, g, 0)
            pe.wait_ge(wlo_done, 3)

            def image(i, last):
                for q in range(PAIRS):
                    final = last and q == PAIRS - 1
                    for e in range(STEPS):
                        l = q * STEPS + e
                        g, p = IMG * i + l, PAIRS * i + q
                        la = (l + LEAD) % IMG
                        if not (last and l + LEAD >= IMG):
                            scores(g + LEAD, la, p + (1 if e + LEAD >= STEPS else 0))
                        if q == 1 and e == TAPS and not last:
                            pe.wait_ge(geps_done, i + 2)
                        outputs(g, l, 2 * p + e // TAPS)
                        if not final:
                            if e == 0:
                                pe.wait_ge(xl_done, p + 2)
                                pe.wait_ge(dsb_done, p + 1)
                            hidden_slots((q + 1) % PAIRS, e * CONV_SLOTS, CONV_SLOTS)
                            if e == 10:
                                tap_products(p + 1)
                        if q == 1 and not last:
                            if e == 3:
                                pe.wait_ge(drained, 4 * p + DR0)
                                group_mean(i + 1)
                            if e == 6:
                                group_var(i + 1)

            with pe.Fori(0, B - 1) as i:
                image(i, False)
            image(B - 1, True)


_OUT_SHAPE = (8, 256, 64, 64)


def kernel(**inputs):
    import numpy as np
    import concourse.bacc as _bacc
    from concourse import mybir as _mybir
    from concourse.bass_utils import run_bass_kernel_spmd as _run

    a = {k.replace("L0_conv_", ""): np.asarray(v) for k, v in inputs.items()}
    x = a["x"]
    H, M, C = 2, a["w_c1"].shape[0], x.shape[1]
    w_d1 = a["w_d1"].reshape(M, H, P, TAPS).transpose(2, 1, 3, 0)
    w_c1 = a["w_c1"].reshape(M, H, P).transpose(2, 1, 0)
    w_out = a["W"].reshape(C, H, P, TAPS).transpose(2, 1, 3, 0)
    tap0 = np.broadcast_to(a["w_d2"][0][:, None], (M, C))
    w_s0 = np.stack([np.concatenate([tap0, a["w_c2"].T]), np.concatenate([a["w_c2"].T, tap0])], 1)
    w_d2 = np.zeros((P, 2, D_ROWS), np.float32)
    vecs = np.zeros((P, 6), np.float32)
    delta = np.zeros((D_ROWS, TAPS - 1, P), np.float16)
    for r in (0, 32, 64):
        w_d2[0:M, 0, r:r + TAPS] = a["w_d2"].T
        w_d2[M:2 * M, 1, r:r + TAPS] = a["w_d2"].T
        vecs[r:r + TAPS, 4] = a["b_d2"]
        for k in range(TAPS - 1):
            delta[r + k + 1, k] = 1
            delta[r + k, k] = -1
    vecs[:, 0] = np.concatenate([a["b_d1"], a["b_c1"]])
    vecs[:, 1] = np.concatenate([a["b_c1"], a["b_d1"]])
    vecs[:, 2] = a["b_c2"][0:P]
    vecs[:, 3] = a["b_c2"][P:2 * P]
    vecs[:, 5] = a["b_d2"][0]
    group_avg = np.kron(np.eye(P // GROUP, dtype=np.float32), np.full((GROUP, GROUP), 1.0 / GROUP, np.float32))

    nc = _bacc.Bacc("TRN2", target_bir_lowering=False, num_devices=1)
    arrays, args = {}, []
    for name, v in (("x", x), ("w_d1", w_d1), ("w_c1", w_c1), ("w_out", w_out), ("w_s0", w_s0), ("w_d2", w_d2),
                    ("vecs", vecs), ("delta", delta), ("group_avg", group_avg)):
        v = np.ascontiguousarray(v)
        arrays[f"in_{name}_dram"] = v
        args.append(nc.dram_tensor(f"in_{name}_dram", v.shape, _mybir.dt.from_np(v.dtype), kind="ExternalInput").ap())
    args.append(nc.dram_tensor("out_0_dram", _OUT_SHAPE, _mybir.dt.float32, kind="ExternalOutput").ap())
    build(nc, *args)
    r = _run(nc, [arrays], core_ids=[0])
    return r.results[0]["out_0_dram"]
```

```python
from contextlib import ExitStack

import concourse.bass as bass
from concourse import mybir

F32 = mybir.dt.float32
F16 = mybir.dt.float16
BF16 = mybir.dt.bfloat16
I32 = mybir.dt.int32
ALU = mybir.AluOpType
ACT = mybir.ActivationFunctionType
AX = mybir.AxisListType

P = 128
TAPS = 9
GROUP = 8
X_SCALE = 128.0
W_TOP = 2.0 ** 14
W_TINY = 1e-30
EPS = 1e-5
D_ROWS = 73
LEAD = 4
ROLL = 5
DRAIN_AT = 4
STATS_AT = 8
ROWS_HIGH_AT = (7, 8, 9, 11)
XT_SLOTS = 3
CONV_SLOTS = 6


def build(nc, x, w_d1, w_c1, w_out, w_s0, w_d2, vecs, delta, group_avg, row_mix, out):
    B, C, R, COLS = x.shape
    H = C // P
    M = w_d1.shape[-1]
    BR = 512 // COLS
    N = BR * COLS
    PAIRS = R // (2 * BR)
    PR = 2 * BR
    SR, SC = PR + 2, COLS + 2
    STEPS = 2 * TAPS
    IMG = PAIRS * STEPS
    CHUNKS = H * R * COLS // 512
    WIN = 4
    assert H == 2 and M == 64 and N == 512 and IMG % 4 == 0 and PAIRS == 4

    x_v = x.rearrange("b (h p) (q r) c -> b q p h (r c)", p=P, q=PAIRS)
    out_v = out.rearrange("b (h p) (q r) c -> b q p h (r c)", p=P, q=PAIRS)

    with ExitStack() as ctx:
        def sb(name, shape, dt=F32):
            return ctx.enter_context(nc.sbuf_tensor(name, shape, dt))

        def ps(name, shape):
            return ctx.enter_context(nc.psum_tensor(name, shape, F32))

        def sem(name):
            return ctx.enter_context(nc.semaphore(name))

        xraw = sb("xraw", [P, H, R * COLS])
        xn = sb("xn", [P, PAIRS, H, SR, SC])
        xt = sb("xt", [P, XT_SLOTS, H, BR, SC])
        xth = sb("xth", [P, 2, WIN, H, BR, SC], F16)
        xtl = sb("xtl", [P, 2, WIN, H, BR, SC], F16)
        xch = sb("xch", [P, H, PR, COLS], F16)
        xcl = sb("xcl", [P, H, PR, COLS], F16)
        wh = sb("wh", [P, H, TAPS, C], F16)
        wl = sb("wl", [P, H, TAPS, C], F16)
        wdh = sb("wdh", [P, WIN, H, 3, M], F16)
        wdl = sb("wdl", [P, WIN, H, 3, M], F16)
        wch = sb("wch", [P, H, M], F16)
        wcl = sb("wcl", [P, H, M], F16)
        ws0 = sb("ws0", [P, 2, C])
        wd2 = sb("wd2", [P, 2, D_ROWS])
        dsel = sb("dsel", [D_ROWS, TAPS - 1, P], BF16)
        rmix = sb("rmix", [P, P])
        m12 = sb("m12", [P, N])
        gavg = sb("gavg", [P, P])
        vec = sb("vec", [P, 6])
        tbias = sb("tbias", [P, H])
        wmax = sb("wmax", [P, 3])
        wmaxall = sb("wmaxall", [P, 3])
        wexp = sb("wexp", [P, 3])
        wtmp = sb("wtmp", [P, 3])
        wscale = sb("wscale", [P, 3])
        wdescale = sb("wdescale", [P, 3])
        yscale = sb("yscale", [P, 2])
        bnst = sb("bnst", [P, H, CHUNKS // H, 6])
        chan = sb("chan", [P, H, 2])
        gmean = sb("gmean", [P, H])
        gdev = sb("gdev", [P, H])
        gdev2 = sb("gdev2", [P, H])
        gsq = sb("gsq", [P, H])
        gvar = sb("gvar", [P, H])
        ghalf = sb("ghalf", [P, H])
        grs = sb("grs", [P, H])
        gn1 = sb("gn1", [P, H])
        gn2 = sb("gn2", [P, H])
        gn3 = sb("gn3", [P, H])
        rstd = sb("rstd", [P, H])
        y = sb("y", [P, 2, N])
        dsb = sb("dsb", [D_ROWS, 2, N])
        dsel16 = dsb[:, 0, :].bitcast(F16).rearrange("p (k c) -> p k c", c=P)
        dpart = sb("dpart", [D_ROWS, 2, 2, N], BF16)
        t = sb("t", [P, 2, H, N])
        u = sb("u", [P, 2, H, N])
        uh = sb("uh", [P, 4, H, N], F16)
        ul = sb("ul", [P, 4, H, N], F16)
        osb = sb("osb", [P, H, 2 * N])

        acc = ps("acc", [P, 2, 2, N])
        sc = ps("sc", [P, H, N])
        yp = ps("yp", [P, 2, N])

        nW, nD, nC, nR = H * TAPS * C, H * TAPS * M, H * M, H * 3 * M
        spare = t[:].rearrange("p a h n -> p (a h n)")
        spare2 = u[:].rearrange("p a h n -> p (a h n)")
        wraw = spare[:, 0:nD]
        wf_c1 = spare[:, nD:nD + nC]
        half_g1 = spare[:, nD + nC:nD + nC + nR]
        wcomb = spare2[:, 0:WIN * nR]
        g02 = spare2[:, WIN * nR:WIN * nR + nR]
        wf_out = xn[:, 2:4].rearrange("p q h r c -> p (q h r c)")[:, 0:nW]
        wf = [wraw, wf_c1, wf_out]
        ws = [wcomb, wf_c1, wf_out]
        w_hi = [wdh[:].rearrange("p w h k m -> p (w h k m)"), wch[:].rearrange("p h m -> p (h m)"),
                wh[:].rearrange("p h k m -> p (h k m)")]
        w_lo = [wdl[:].rearrange("p w h k m -> p (w h k m)"), wcl[:].rearrange("p h m -> p (h m)"),
                wl[:].rearrange("p h k m -> p (h k m)")]

        x_loaded = [sem(f"x_loaded{q}") for q in range(PAIRS)]
        w_loaded = [sem(f"w_loaded{n}") for n in range(3)]
        c_loaded = sem("c_loaded")
        zeroed = sem("zeroed")
        wmax_done = sem("wmax_done")
        wred_done = sem("wred_done")
        wscale_done = sem("wscale_done")
        whi_done = sem("whi_done")
        wlo_done = sem("wlo_done")
        const_done = sem("const_done")
        chain = sem("chain")
        bn_done = sem("bn_done")
        chan_done = sem("chan_done")
        gmean_done = sem("gmean_done")
        gcopy_done = sem("gcopy_done")
        gdev_done = sem("gdev_done")
        gsq_done = sem("gsq_done")
        gvar_done = sem("gvar_done")
        geps_done = sem("geps_done")
        gpow_done = sem("gpow_done")
        gnewton = sem("gnewton")
        xn_done = sem("xn_done")
        xt_done = sem("xt_done")
        xth_done = sem("xth_done")
        xtl_done = sem("xtl_done")
        xch_done = sem("xch_done")
        xcl_done = sem("xcl_done")
        res_loaded = sem("res_loaded")
        m_done = sem("m_done")
        m12_done = sem("m12_done")
        conv_done = sem("conv_done")
        y_done = sem("y_done")
        d_done = sem("d_done")
        dsb_done = sem("dsb_done")
        dstep = sem("dstep")
        dpart_done = sem("dpart_done")
        s_done = sem("s_done")
        t_done = sem("t_done")
        u_done = sem("u_done")
        hi_done = sem("hi_done")
        lo_done = sem("lo_done")
        used = sem("used")
        drained = sem("drained")
        stored = sem("stored")

        U0, HI0, LO0, USED0, DR0, ST0 = 4, 2, 2, 4, 4, 16

        block = ctx.enter_context(nc.Block())

        def pairs_of(q):
            return (1 if q == 0 else 0), (SR - 1 if q == PAIRS - 1 else SR)

        @block.sync
        def _(sp):
            sp.sem_inc(stored, ST0)
            sp.dma_start(wf[0], w_d1.rearrange("p h k m -> p (h k m)")).then_inc(w_loaded[0], 16)
            sp.dma_start(wf[1], w_c1.rearrange("p h m -> p (h m)")).then_inc(w_loaded[1], 16)

            def load_image(image):
                for q in range(PAIRS):
                    sp.dma_start(xraw[:, :, q * PR * COLS:(q + 1) * PR * COLS],
                                 x_v[image, q]).then_inc(x_loaded[q], 16)

            load_image(0)
            sp.dma_start(wf[2], w_out.rearrange("p h k m -> p (h k m)")).then_inc(w_loaded[2], 16)
            sp.dma_start(osb[:], x_v[0, 0]).then_inc(res_loaded, 16)

            def image(i, last):
                if not last:
                    sp.wait_ge(xn_done, PAIRS * i + PAIRS)
                    load_image(i + 1)
                for q in range(PAIRS):
                    sp.wait_ge(drained, 4 * (PAIRS * i + q) + 4 + DR0)
                    sp.dma_start(out_v[i, q], osb[:]).then_inc(stored, 16)
                    if not (last and q == PAIRS - 1):
                        sp.wait_ge(stored, 16 * (PAIRS * i + q + 1) + ST0)
                        sp.dma_start(osb[:], x_v[i, q + 1] if q < PAIRS - 1 else
                                     x_v[i + 1, 0]).then_inc(res_loaded, 16)

            with sp.Fori(0, B - 1) as i:
                image(i, False)
            image(B - 1, True)
            sp.wait_ge(stored, 16 * B * PAIRS + ST0)

        def row_window(eng, p, q, c):
            first, second, op = ((0, 2, ALU.subtract), (1, 2, ALU.add), (2, 1, ALU.subtract),
                                 (3, 1, ALU.subtract))[c]
            return eng.tensor_tensor(xt[:, c % XT_SLOTS], xn[:, q, :, first:first + 2 * BR - 1:2, :],
                                     xn[:, q, :, second:second + 2 * BR - 1:2, :], op).then_inc(xt_done, 1)

        def row_window_low(eng, q, c):
            def flat(a):
                return a.rearrange("p h r c -> p (h r c)")
            return eng.tensor_tensor(flat(xtl[:, q % 2, c]), flat(xt[:, c % XT_SLOTS]), flat(xth[:, q % 2, c]),
                                     ALU.subtract).then_inc(xtl_done, 1)

        def inside(q):
            return xn[:, q, :, 1:1 + PR, 1:1 + COLS]

        @block.gpsimd
        def _(pool):
            nc.gpsimd.memset(ghalf[:], -0.5)
            nc.gpsimd.memset(xn[:, 0:2], 0.0).then_inc(zeroed, 1)

            def tensor_max(n):
                pool.wait_ge(wmax_done, n + 1)
                nc.gpsimd.partition_all_reduce(wmaxall[:, n:n + 1], wmax[:, n:n + 1], P,
                                               bass.bass_isa.ReduceOp.max).then_inc(wred_done, 1)

            def root(image):
                pool.wait_ge(geps_done, image + 1)
                nc.gpsimd.tensor_tensor(grs[:], gvar[:], ghalf[:], ALU.pow).then_inc(gpow_done, 1)

            def split_rows(p, q):
                pool.wait_ge(xn_done, p + 1)

                def low_part(c):
                    pool.wait_ge(xt_done, WIN * p + c + 1)
                    pool.wait_ge(xth_done, WIN * p + c + 1)
                    row_window_low(nc.gpsimd, q, c)

                for c in range(WIN):
                    if c < XT_SLOTS:
                        pool.wait_ge(xtl_done, WIN * p)
                    else:
                        low_part(c - XT_SLOTS)
                        pool.wait_ge(xtl_done, WIN * p + c - XT_SLOTS + 1)
                    row_window(nc.gpsimd, p, q, c)
                for c in range(WIN - XT_SLOTS, WIN):
                    low_part(c)
                pool.wait_ge(xch_done, p + 1)
                nc.gpsimd.tensor_tensor(xcl[:], inside(q), xch[:], ALU.subtract).then_inc(xcl_done, 1)

            tensor_max(0)
            tensor_max(1)
            root(0)
            tensor_max(2)
            pool.wait_ge(wlo_done, 3)
            nc.gpsimd.memset(xn[:, 2:4], 0.0).then_inc(zeroed, 1)
            split_rows(1, 1)

            with pool.Fori(0, B - 1) as i:
                split_rows(PAIRS * i + 2, 2)
                split_rows(PAIRS * i + 3, 3)
                root(i + 1)
                split_rows(PAIRS * i + 4, 0)
                split_rows(PAIRS * i + 5, 1)
            split_rows(PAIRS * (B - 1) + 2, 2)
            split_rows(PAIRS * (B - 1) + 3, 3)

        @block.scalar
        def _(act):
            act.dma_start(vec[:], vecs).then_inc(c_loaded, 16)
            act.dma_start(gavg[:], group_avg).then_inc(c_loaded, 16)
            act.dma_start(ws0[:], w_s0).then_inc(c_loaded, 16)
            act.dma_start(wd2[:], w_d2).then_inc(c_loaded, 16)
            act.dma_start(dsel16, delta).then_inc(c_loaded, 16)
            act.dma_start(rmix[:], row_mix).then_inc(c_loaded, 16)

            def weights_high(n):
                act.wait_ge(w_loaded[n], 16)
                act.wait_ge(wscale_done, n + 1)
                nc.scalar.activation(w_hi[n], ws[n], ACT.Copy, scale=wscale[:, n:n + 1]).then_inc(whi_done, 1)

            def tanh(g, l):
                for h in range(H):
                    act.wait_ge(s_done, 2 * g + h + 1)
                    act.wait_ge(u_done, 2 * (g - 2) + h + 1 + U0)
                    nc.scalar.activation(t[:, l % 2, h, :], sc[:, h, :], ACT.Tanh,
                                         bias=tbias[:, h:h + 1]).then_inc(t_done, 1)

            def high(g, l):
                act.wait_ge(u_done, 2 * g + 2 + U0)
                act.wait_ge(used, g - 3 + USED0)
                nc.scalar.activation(uh[:, l % 4, :, :], u[:, l % 2, :, :], ACT.Copy).then_inc(hi_done, 1)

            def rows_high(p, q, c):
                act.wait_ge(xt_done, WIN * p + c + 1)
                nc.scalar.activation(xth[:, q % 2, c].rearrange("p h r c -> p (h r c)"),
                                     xt[:, c % XT_SLOTS].rearrange("p h r c -> p (h r c)"), ACT.Copy).then_inc(xth_done, 1)

            def x_high(p, q):
                act.wait_ge(xn_done, p + 1)
                nc.scalar.activation(xch[:], inside(q), ACT.Copy).then_inc(xch_done, 1)

            def keep_m12(p):
                act.wait_ge(m_done, p + 1)
                nc.scalar.activation(m12[:], yp[:, 1, :], ACT.Copy).then_inc(m12_done, 1)

            def hidden(p):
                act.wait_ge(conv_done, p + 1)
                for b in range(2):
                    for half in range(2):
                        rows = slice(M * half, M * half + M)
                        ins = nc.scalar.activation(y[rows, b, :], yp[rows, 0 if half == b else 1, :], ACT.Relu,
                                                   bias=vec[rows, b:b + 1], scale=yscale[rows, b:b + 1])
                ins.then_inc(y_done, 1)

            def tap_bias(p):
                act.wait_ge(d_done, p + 1)
                nc.scalar.activation(dsb[:], yp[0:D_ROWS, :, :], ACT.Identity,
                                     bias=vec[0:D_ROWS, 4:5]).then_inc(dsb_done, 1)

            act.wait_ge(c_loaded, 6 * 16)
            act.wait_ge(zeroed, 1)
            weights_high(0)
            weights_high(1)
            for c in range(WIN):
                rows_high(0, 0, c)
            x_high(0, 0)
            weights_high(2)
            act.wait_ge(const_done, 1)
            keep_m12(0)
            hidden(0)
            tap_bias(0)
            for c in range(WIN):
                rows_high(1, 1, c)
            x_high(1, 1)

            def step(i, l, last):
                q, e = divmod(l, STEPS)
                g, p = IMG * i + l, PAIRS * i + q
                tanh(g, l)
                if not (isinstance(g, int) and g == 0):
                    high(g - 1, (l - 1) % IMG)
                if not (last and q >= PAIRS - 2):
                    if e in ROWS_HIGH_AT:
                        rows_high(p + 2, (q + 2) % PAIRS, ROWS_HIGH_AT.index(e))
                    if e == 15:
                        x_high(p + 2, (q + 2) % PAIRS)
                if e == 10 and not (last and q == PAIRS - 1):
                    keep_m12(p + 1)
                if e == 13 and not (last and q == PAIRS - 1):
                    hidden(p + 1)
                if e == 14 and not (last and q == PAIRS - 1):
                    tap_bias(p + 1)

            for l in range(ROLL):
                step(0, l, False)
            with act.Fori(0, B - 1) as i:
                for l in range(ROLL, IMG):
                    step(i, l, False)
                for l in range(ROLL):
                    step(i + 1, l, False)
            for l in range(ROLL, IMG):
                step(B - 1, l, True)
            high(B * IMG - 1, IMG - 1)

        @block.vector
        def _(dve):
            for s, n in ((u_done, U0), (hi_done, HI0), (lo_done, LO0), (drained, DR0)):
                dve.sem_inc(s, n)
            links = [0]

            def link(ins):
                links[0] += 1
                ins.then_inc(chain, 1)
                dve.wait_ge(chain, links[0])

            def weight_scale(n):
                dve.wait_ge(w_loaded[n], 16)
                nc.vector.tensor_reduce(wmax[:, n:n + 1], wf[n], AX.X, ALU.max,
                                        apply_absolute_value=True).then_inc(wmax_done, 1)

            def weight_scale_2(n):
                dve.wait_ge(wred_done, n + 1)
                c = slice(n, n + 1)
                link(nc.vector.tensor_scalar(wtmp[:, c], wmaxall[:, c], W_TINY, None, ALU.max))
                link(nc.vector.tensor_scalar(wexp[:, c].bitcast(I32), wtmp[:, c].bitcast(I32), 0x7F800000, None,
                                             ALU.bitwise_and))
                link(nc.vector.tensor_scalar(wtmp[:, c], wexp[:, c], 1.0 / W_TOP, None, ALU.mult))
                link(nc.vector.tensor_scalar(wdescale[:, c], wexp[:, c], 1.0 / (W_TOP * X_SCALE), None, ALU.mult))
                nc.vector.reciprocal(wscale[:, c], wtmp[:, c]).then_inc(wscale_done, 1)

            def combine_rows():
                g = wraw.rearrange("p (h y k) -> p y h k", h=H, y=3)
                def part(a):
                    return a.rearrange("p (h k) -> p h k", h=H)
                out = [part(wcomb[:, nR * c:nR * (c + 1)]) for c in range(WIN)]
                nc.vector.tensor_copy(out[0], g[:, 0])
                nc.vector.tensor_copy(out[3], g[:, 2])
                nc.vector.tensor_scalar(part(half_g1), g[:, 1], 0.5, None, ALU.mult)
                link(nc.vector.tensor_tensor(part(g02), g[:, 0], g[:, 2], ALU.add))
                for c, op in ((1, ALU.add), (2, ALU.subtract)):
                    ins = nc.vector.scalar_tensor_tensor(out=out[c], in0=part(g02), scalar=0.5, in1=part(half_g1),
                                                         op0=ALU.mult, op1=op)
                link(ins)

            def weights_low(n):
                dve.wait_ge(whi_done, n + 1)
                dve.wait_ge(wscale_done, n + 1)
                nc.vector.scalar_tensor_tensor(out=w_lo[n], in0=ws[n], scalar=wscale[:, n:n + 1], in1=w_hi[n],
                                               op0=ALU.mult, op1=ALU.subtract).then_inc(wlo_done, 1)

            def stats(image, c):
                q, r = divmod(c, CHUNKS // PAIRS)
                h, k = divmod(r, CHUNKS // PAIRS // H)
                n = q * (CHUNKS // PAIRS // H) + k
                if r == 0:
                    dve.wait_ge(x_loaded[q], 16 * image + 16)
                ins = nc.vector.bn_stats(bnst[:, h, n, :], xraw[:, h, 512 * n:512 * n + 512])
                if c == CHUNKS - 1:
                    ins.then_inc(bn_done, 1)

            def chan_stats(image):
                for h in range(H):
                    ins = nc.vector.bn_aggr(chan[:, h, :], bnst[:, h].rearrange("p n s -> p (n s)"))
                ins.then_inc(chan_done, 1)

            def group_dev(image):
                dve.wait_ge(gmean_done, image + 1)
                nc.vector.tensor_copy(gmean[:], acc[:, 0, 0, 0:H]).then_inc(gcopy_done, 1)
                dve.wait_ge(gcopy_done, image + 1)
                nc.vector.tensor_tensor(gdev[:], chan[:, :, 0], gmean[:], ALU.subtract).then_inc(gdev_done, 1)
                dve.wait_ge(gdev_done, 2 * image + 1)
                nc.vector.tensor_tensor(gdev2[:], gdev[:], gdev[:], ALU.mult).then_inc(gdev_done, 1)
                dve.wait_ge(gdev_done, 2 * image + 2)
                nc.vector.tensor_tensor(gsq[:], gdev2[:], chan[:, :, 1], ALU.add).then_inc(gsq_done, 1)

            def group_eps(image):
                dve.wait_ge(gvar_done, image + 1)
                nc.vector.tensor_scalar(gvar[:], acc[:, 0, 0, 0:H], EPS, None, ALU.add).then_inc(geps_done, 1)

            def group_root(image):
                dve.wait_ge(gpow_done, image + 1)
                nc.vector.tensor_tensor(gn1[:], grs[:], grs[:], ALU.mult).then_inc(gnewton, 1)
                dve.wait_ge(gnewton, 4 * image + 1)
                nc.vector.tensor_tensor(gn2[:], gn1[:], gvar[:], ALU.mult).then_inc(gnewton, 1)
                dve.wait_ge(gnewton, 4 * image + 2)
                nc.vector.tensor_scalar(gn3[:], gn2[:], -0.5 * X_SCALE, 1.5 * X_SCALE, ALU.mult,
                                        ALU.add).then_inc(gnewton, 1)
                dve.wait_ge(gnewton, 4 * image + 3)
                nc.vector.tensor_tensor(rstd[:], grs[:], gn3[:], ALU.mult).then_inc(gnewton, 1)

            def normalise(image, p, q):
                dve.wait_ge(gnewton, 4 * image + 4)
                r0, r1 = pairs_of(q)
                for h in range(H):
                    src = xraw[:, h, (q * PR - 1 + r0) * COLS:(q * PR - 1 + r1) * COLS]
                    ins = nc.vector.tensor_scalar(xn[:, q, h, r0:r1, 1:1 + COLS],
                                                  src.rearrange("p (r c) -> p r c", c=COLS),
                                                  gmean[:, h:h + 1], rstd[:, h:h + 1], ALU.subtract, ALU.mult)
                ins.then_inc(xn_done, 1)

            def split_taps(p, q):
                d = dpart[:, q % 2]
                dve.wait_ge(dsb_done, p + 1)
                nc.vector.tensor_copy(d, dsb[:]).then_inc(dstep, 1)
                dve.wait_ge(dstep, 3 * p + 1)
                nc.vector.tensor_tensor(dsb[:], dsb[:], d, ALU.subtract).then_inc(dstep, 1)

            def split_taps_2(p, q):
                d = dpart[:, q % 2]
                dve.wait_ge(dstep, 3 * p + 2)
                nc.vector.tensor_copy(d[0:32 + TAPS], dsb[0:32 + TAPS]).then_inc(dstep, 1)
                dve.wait_ge(dstep, 3 * p + 3)
                nc.vector.tensor_tensor(d[0:TAPS], dsb[0:TAPS], d[0:TAPS], ALU.subtract).then_inc(dpart_done, 1)

            def gate(g, l):
                q, e = divmod(l, STEPS)
                b, k = divmod(e, TAPS)
                dy, dx = divmod(k, 3)
                dve.wait_ge(hi_done, g - 1 + HI0)
                dve.wait_ge(lo_done, g - 1 + LO0)
                for h in range(H):
                    dve.wait_ge(t_done, 2 * g + h + 1)
                    nc.vector.scalar_tensor_tensor(
                        out=u[:, l % 2, h, :].rearrange("p (r c) -> p r c", c=COLS),
                        in0=t[:, l % 2, h, :].rearrange("p (r c) -> p r c", c=COLS), scalar=1.0,
                        in1=xn[:, q, h, b + dy:b + dy + PR - 1:2, dx:dx + COLS],
                        op0=ALU.add, op1=ALU.mult).then_inc(u_done, 1)

            def low(g, l):
                dve.wait_ge(hi_done, g + 1 + HI0)
                nc.vector.tensor_tensor(ul[:, l % 4, :, :], u[:, l % 2, :, :], uh[:, l % 4, :, :],
                                        ALU.subtract).then_inc(lo_done, 1)

            def drain(p, b):
                dve.wait_ge(used, TAPS * (2 * p + b + 1) + USED0)
                dve.wait_ge(res_loaded, 16 * p + 16)
                for m in range(H):
                    rows = osb[:, m].rearrange("p (j b c) -> p b j c", b=2, c=COLS)[:, b]
                    nc.vector.scalar_tensor_tensor(
                        out=rows, in0=acc[:, b, m, :].rearrange("p (r c) -> p r c", c=COLS),
                        scalar=wdescale[:, 2:3], in1=rows, op0=ALU.mult, op1=ALU.add).then_inc(drained, 1)

            weight_scale(0)
            weight_scale(1)
            combine_rows()
            weight_scale_2(0)
            weight_scale_2(1)
            dve.wait_ge(c_loaded, 6 * 16)
            for b in range(2):
                for half, n in ((b, 0), (1 - b, 1)):
                    rows = slice(M * half, M * half + M)
                    nc.vector.tensor_copy(yscale[rows, b:b + 1], wdescale[rows, n:n + 1])
            for h in range(H):
                nc.vector.tensor_tensor(tbias[:, h:h + 1], vec[:, 2 + h:3 + h], vec[:, 5:6], ALU.add)
            nc.vector.tensor_copy(dsel[:], dsel16).then_inc(const_done, 1)
            weights_low(0)
            weights_low(1)
            for c in range(CHUNKS):
                stats(0, c)
            dve.wait_ge(bn_done, 1)
            chan_stats(0)
            group_dev(0)
            group_eps(0)
            group_root(0)
            dve.wait_ge(zeroed, 1)
            normalise(0, 0, 0)
            dve.wait_ge(xn_done, 1)
            for c in range(XT_SLOTS):
                row_window(nc.vector, 0, 0, c)
            for c in range(WIN):
                dve.wait_ge(xt_done, c + 1)
                dve.wait_ge(xth_done, c + 1)
                row_window_low(nc.vector, 0, c)
                if c + XT_SLOTS < WIN:
                    dve.wait_ge(xtl_done, c + 1)
                    row_window(nc.vector, 0, 0, c + XT_SLOTS)
            normalise(0, 1, 1)
            dve.wait_ge(xch_done, 1)
            nc.vector.tensor_tensor(xcl[:], inside(0), xch[:], ALU.subtract).then_inc(xcl_done, 1)
            weight_scale(2)
            weight_scale_2(2)
            weights_low(2)
            split_taps(0, 0)
            split_taps_2(0, 0)

            def step(i, l, last):
                q, e = divmod(l, STEPS)
                g, p = IMG * i + l, PAIRS * i + q
                if e == 0:
                    dve.wait_ge(xn_done, p + 1)
                if q == 1 and e == STATS_AT + CHUNKS // 2 and not last:
                    dve.wait_ge(bn_done, i + 2)
                gate(g, l)
                if not (isinstance(g, int) and g == 0):
                    low(g - 1, (l - 1) % IMG)
                if e == 1 and q < 2:
                    if isinstance(i, int) and i == 0:
                        dve.wait_ge(zeroed, 2)
                    normalise(i, p + 2, q + 2)
                if e == 4 and q >= 2 and not last:
                    normalise(i + 1, p + 2, q - 2)
                if e == DRAIN_AT and not (isinstance(p, int) and p == 0):
                    drain(p - 1, 1)
                if e == TAPS + DRAIN_AT:
                    drain(p, 0)
                if e == 15 and not (last and q == PAIRS - 1):
                    split_taps(p + 1, q + 1)
                if e == 16 and not (last and q == PAIRS - 1):
                    split_taps_2(p + 1, q + 1)
                if not last:
                    if q == 1 and STATS_AT <= e < STATS_AT + CHUNKS // 2:
                        stats(i + 1, 2 * (e - STATS_AT))
                        stats(i + 1, 2 * (e - STATS_AT) + 1)
                    if q == 1 and e == STATS_AT + CHUNKS // 2:
                        chan_stats(i + 1)
                    if q == 2 and e == 0:
                        group_dev(i + 1)
                    if q == 2 and e == 2:
                        group_eps(i + 1)
                    if q == 2 and e == 3:
                        group_root(i + 1)

            for l in range(ROLL):
                step(0, l, False)
            with dve.Fori(0, B - 1) as i:
                for l in range(ROLL, IMG):
                    step(i, l, False)
                for l in range(ROLL):
                    step(i + 1, l, False)
            for l in range(ROLL, IMG):
                step(B - 1, l, True)
            low(B * IMG - 1, IMG - 1)
            drain(PAIRS * B - 1, 1)

        @block.tensor
        def _(pe):
            pe.sem_inc(used, USED0)

            def scores(g, l, p):
                q, e = divmod(l, STEPS)
                b, k = divmod(e, TAPS)
                if k == 0 and b == 0:
                    pe.wait_ge(y_done, p + 1)
                if k == 1 and b == 0:
                    pe.wait_ge(dpart_done, p + 1)
                for h in range(H):
                    if not (isinstance(g, int) and g == 0):
                        pe.wait_ge(t_done, 2 * (g - 1) + h + 1)
                    if k == 0:
                        ins = nc.tensor.matmul(sc[:, h, :], ws0[:, b, h * P:(h + 1) * P], y[:, b, :],
                                               start=True, stop=True)
                    else:
                        ins = nc.tensor.matmul(sc[:, h, :], dsel[:, k - 1, :], dpart[:, q % 2, b, :],
                                               start=False, stop=True, skip_group_check=True)
                    ins.then_inc(s_done, 1)

            def outputs(g, l, n):
                b, k = divmod(l % STEPS, TAPS)
                pe.wait_ge(lo_done, g + 1 + LO0)
                if k == 0:
                    pe.wait_ge(drained, 2 * (n - 1) + DR0)
                for h in range(H):
                    for m in range(H):
                        cols = slice(m * P, (m + 1) * P)
                        for j, (w, v) in enumerate(((wh, uh), (wh, ul), (wl, uh))):
                            ins = nc.tensor.matmul(acc[:, b, m, :], w[:, h, k, cols], v[:, l % 4, h, :],
                                                   start=(k == 0 and h == 0 and j == 0),
                                                   stop=(k == TAPS - 1 and h == H - 1 and j == 2))
                ins.then_inc(used, 1)

            slots = [(pair, h, k, j) for pair in ((0, 3), (1, 2)) for h in range(H) for k in range(3)
                     for j in range(3)]

            def conv_slots(p, q, first, count):
                for s in range(first, min(first + count, len(slots))):
                    pair, h, k, j = slots[s]
                    for half, c in enumerate(pair):
                        ins = nc.tensor.matmul(
                            yp[M * half:M * half + M, 0 if pair[0] == 0 else 1, :],
                            (wdh, wdh, wdl)[j][:, c, h, k, :],
                            (xth, xtl, xth)[j][:, q % 2, c, h, :, k:k + COLS],
                            start=(h == 0 and k == 0 and j == 0), stop=(h == H - 1 and k == 2 and j == 2))
                    if s == len(slots) - 1:
                        ins.then_inc(m_done, 1)

            def row_sums(p):
                pe.wait_ge(m12_done, p + 1)
                nc.tensor.matmul(yp[:, 0, :], rmix[:], m12[:], start=False, stop=True, skip_group_check=True)

            def channel_slots(p, h):
                if h == 0:
                    pe.wait_ge(xcl_done, p + 1)
                for j in range(3):
                    for half in range(2):
                        ins = nc.tensor.matmul(
                            yp[M * half:M * half + M, 1, :], (wch, wch, wcl)[j][:, h, :],
                            (xch, xcl, xch)[j][:, h, 1 - half:PR:2, :],
                            start=(h == 0 and j == 0), stop=(h == H - 1 and j == 2))
                if h == H - 1:
                    ins.then_inc(conv_done, 1)

            def tap_products(p):
                pe.wait_ge(y_done, p + 1)
                for b in range(2):
                    ins = nc.tensor.matmul(yp[0:D_ROWS, b, :], wd2[:, b, :], y[:, b, :], start=True, stop=True)
                ins.then_inc(d_done, 1)

            def group_mean(image):
                pe.wait_ge(chan_done, image + 1)
                nc.tensor.matmul(acc[:, 0, 0, 0:H], gavg[:], chan[:, :, 0], start=True,
                                 stop=True).then_inc(gmean_done, 1)

            def group_var(image):
                pe.wait_ge(gsq_done, image + 1)
                nc.tensor.matmul(acc[:, 0, 0, 0:H], gavg[:], gsq[:], start=True, stop=True).then_inc(gvar_done, 1)

            pe.wait_ge(c_loaded, 6 * 16)
            group_mean(0)
            group_var(0)
            pe.wait_ge(wlo_done, 2)
            pe.wait_ge(xtl_done, WIN)
            conv_slots(0, 0, 0, len(slots))
            row_sums(0)
            channel_slots(0, 0)
            channel_slots(0, 1)
            tap_products(0)
            pe.wait_ge(const_done, 1)
            for g in range(LEAD):
                scores(g, g, 0)
            pe.wait_ge(wlo_done, 3)

            def image(i, last):
                for q in range(PAIRS):
                    final = last and q == PAIRS - 1
                    for e in range(STEPS):
                        l = q * STEPS + e
                        g, p = IMG * i + l, PAIRS * i + q
                        la = (l + LEAD) % IMG
                        if not (last and l + LEAD >= IMG):
                            scores(g + LEAD, la, p + (1 if e + LEAD >= STEPS else 0))
                        if q == 2 and e == 0 and not last:
                            pe.wait_ge(geps_done, i + 2)
                        outputs(g, l, 2 * p + e // TAPS)
                        if not final:
                            if e == 0:
                                pe.wait_ge(xtl_done, WIN * (p + 2))
                                pe.wait_ge(dsb_done, p + 1)
                            conv_slots(p + 1, (q + 1) % PAIRS, e * CONV_SLOTS, CONV_SLOTS)
                            if e == 7:
                                row_sums(p + 1)
                            if e in (7, 8):
                                channel_slots(p + 1, e - 7)
                            if e == 10:
                                tap_products(p + 1)
                        if q == 1 and not last:
                            if e == 14:
                                pe.wait_ge(drained, 4 * p + 2 + DR0)
                                group_mean(i + 1)
                            if e == 16:
                                group_var(i + 1)

            with pe.Fori(0, B - 1) as i:
                image(i, False)
            image(B - 1, True)


_OUT_SHAPE = (8, 256, 64, 64)


def kernel(**inputs):
    import numpy as np
    import concourse.bacc as _bacc
    from concourse import mybir as _mybir
    from concourse.bass_utils import run_bass_kernel_spmd as _run

    a = {k.replace("L0_conv_", ""): np.asarray(v) for k, v in inputs.items()}
    x = a["x"]
    H, M, C = 2, a["w_c1"].shape[0], x.shape[1]
    w_d1 = a["w_d1"].reshape(M, H, P, TAPS).transpose(2, 1, 3, 0)
    w_c1 = a["w_c1"].reshape(M, H, P).transpose(2, 1, 0)
    w_out = a["W"].reshape(C, H, P, TAPS).transpose(2, 1, 3, 0)
    tap0 = np.broadcast_to(a["w_d2"][0][:, None], (M, C))
    w_s0 = np.stack([np.concatenate([tap0, a["w_c2"].T]), np.concatenate([a["w_c2"].T, tap0])], 1)
    w_d2 = np.zeros((P, 2, D_ROWS), np.float32)
    vecs = np.zeros((P, 6), np.float32)
    delta = np.zeros((D_ROWS, TAPS - 1, P), np.float16)
    for r in (0, 32, 64):
        w_d2[0:M, 0, r:r + TAPS] = a["w_d2"].T
        w_d2[M:2 * M, 1, r:r + TAPS] = a["w_d2"].T
        vecs[r:r + TAPS, 4] = a["b_d2"]
        for k in range(TAPS - 1):
            delta[r + k + 1, k] = 1
            delta[r + k, k] = -1
    vecs[:, 0] = np.concatenate([a["b_d1"], a["b_c1"]])
    vecs[:, 1] = np.concatenate([a["b_c1"], a["b_d1"]])
    vecs[:, 2] = a["b_c2"][0:P]
    vecs[:, 3] = a["b_c2"][P:2 * P]
    vecs[:, 5] = a["b_d2"][0]
    group_avg = np.kron(np.eye(P // GROUP, dtype=np.float32), np.full((GROUP, GROUP), 1.0 / GROUP, np.float32))

    row_mix = np.kron(np.array([[1, 1], [1, -1]], np.float32), np.eye(M, dtype=np.float32))

    nc = _bacc.Bacc("TRN2", target_bir_lowering=False, num_devices=1)
    arrays, args = {}, []
    for name, v in (("x", x), ("w_d1", w_d1), ("w_c1", w_c1), ("w_out", w_out), ("w_s0", w_s0), ("w_d2", w_d2),
                    ("vecs", vecs), ("delta", delta), ("group_avg", group_avg),
                    ("row_mix", row_mix)):
        v = np.ascontiguousarray(v)
        arrays[f"in_{name}_dram"] = v
        args.append(nc.dram_tensor(f"in_{name}_dram", v.shape, _mybir.dt.from_np(v.dtype), kind="ExternalInput").ap())
    args.append(nc.dram_tensor("out_0_dram", _OUT_SHAPE, _mybir.dt.float32, kind="ExternalOutput").ap())
    build(nc, *args)
    r = _run(nc, [arrays], core_ids=[0])
    return r.results[0]["out_0_dram"]
```

```python
from contextlib import ExitStack

import concourse.bass as bass
from concourse import mybir

F32 = mybir.dt.float32
F16 = mybir.dt.float16
BF16 = mybir.dt.bfloat16
I32 = mybir.dt.int32
ALU = mybir.AluOpType
ACT = mybir.ActivationFunctionType
AX = mybir.AxisListType

P = 128
TAPS = 9
GROUP = 8
X_SCALE = 128.0
W_TOP = 2.0 ** 14
W_TINY = 1e-30
EPS = 1e-5
D_COPIES = 3
LEAD = 4
ROLL = 5
DRAIN_AT = 4
STATS_AT = 8
ROWS_HIGH_AT = (7, 8, 9, 11)
WINDOWS = (0, 3, 1, 2)
M12_AT, HIDDEN_AT, TAP_BIAS_AT = 10, 13, 14
SPLIT_TAPS_AT = 15
X_HIGH_AT = 15
ROW_SUMS_AT, TAP_PRODUCTS_AT = 7, 10
XT_SLOTS = 3
CONV_SLOTS = 6


def build(nc, x, w_d1, w_c1, w_out, w_s0, w_d2, vecs, delta, group_avg, row_mix, out):
    B, C, R, COLS = x.shape
    H = C // P
    M = w_d1.shape[-1]
    BR = 512 // COLS
    N = BR * COLS
    PAIRS = R // (2 * BR)
    PR = 2 * BR
    SR, SC = PR + 2, COLS + 2
    STEPS = 2 * TAPS
    IMG = PAIRS * STEPS
    CHUNKS = H * R * COLS // 512
    WIN = 4
    assert H == 2 and M == 64 and N == 512 and IMG % 4 == 0 and PAIRS == 4

    x_v = x.rearrange("b (h p) (q r) c -> b q p h (r c)", p=P, q=PAIRS)
    out_v = out.rearrange("b (h p) (q r) c -> b q p h (r c)", p=P, q=PAIRS)

    with ExitStack() as ctx:
        def sb(name, shape, dt=F32):
            return ctx.enter_context(nc.sbuf_tensor(name, shape, dt))

        def ps(name, shape):
            return ctx.enter_context(nc.psum_tensor(name, shape, F32))

        def sem(name):
            return ctx.enter_context(nc.semaphore(name))

        xraw = sb("xraw", [P, H, R * COLS])
        xn = sb("xn", [P, PAIRS, H, SR, SC])
        xt = sb("xt", [P, XT_SLOTS, H, BR, SC])
        xth = sb("xth", [P, 2, WIN, H, BR, SC], F16)
        xtl = sb("xtl", [P, 2, WIN, H, BR, SC], F16)
        xch = sb("xch", [P, H, PR, COLS], F16)
        xcl = sb("xcl", [P, H, PR, COLS], F16)
        wh = sb("wh", [P, H, TAPS, C], F16)
        wl = sb("wl", [P, H, TAPS, C], F16)
        wdh = sb("wdh", [P, WIN, H, 3, M], F16)
        wdl = sb("wdl", [P, WIN, H, 3, M], F16)
        wch = sb("wch", [P, H, M], F16)
        wcl = sb("wcl", [P, H, M], F16)
        ws0 = sb("ws0", [P, 2, C])
        wd2 = sb("wd2", [P, 2, M])
        dsel = sb("dsel", [P, 2, TAPS - 1, P], BF16)
        rmix = sb("rmix", [P, P])
        m12 = sb("m12", [P, N])
        gavg = sb("gavg", [P, P])
        vec = sb("vec", [P, 8])
        tbias = sb("tbias", [P, H])
        wmax = sb("wmax", [P, 3])
        wmaxall = sb("wmaxall", [P, 3])
        wexp = sb("wexp", [P, 3])
        wtmp = sb("wtmp", [P, 3])
        wscale = sb("wscale", [P, 3])
        wdescale = sb("wdescale", [P, 3])
        yscale = sb("yscale", [P, 2])
        bnst = sb("bnst", [P, H, CHUNKS // H, 6])
        chan = sb("chan", [P, H, 2])
        gmean = sb("gmean", [P, H])
        gdev = sb("gdev", [P, H])
        gdev2 = sb("gdev2", [P, H])
        gsq = sb("gsq", [P, H])
        gvar = sb("gvar", [P, H])
        ghalf = sb("ghalf", [P, H])
        grs = sb("grs", [P, H])
        gn1 = sb("gn1", [P, H])
        gn2 = sb("gn2", [P, H])
        gn3 = sb("gn3", [P, H])
        rstd = sb("rstd", [P, H])
        y = sb("y", [P, 2, N])
        dsel16 = y[:].rearrange("p b n -> p (b n)").bitcast(F16)
        dsb = sb("dsb", [P, N])
        dhi = sb("dhi", [P, 2, N], BF16)
        dpart = sb("dpart", [P, 2, N], BF16)
        t = sb("t", [P, 2, H, N])
        u = sb("u", [P, 2, H, N])
        uh = sb("uh", [P, 4, H, N], F16)
        ul = sb("ul", [P, 4, H, N], F16)
        osb = sb("osb", [P, H, 2 * N])

        acc = ps("acc", [P, 2, 2, N])
        sc = ps("sc", [P, H, N])
        yp = ps("yp", [P, 2, N])

        nW, nD, nC, nR = H * TAPS * C, H * TAPS * M, H * M, H * 3 * M
        spare = t[:].rearrange("p a h n -> p (a h n)")
        spare2 = u[:].rearrange("p a h n -> p (a h n)")
        wraw = spare[:, 0:nD]
        wf_c1 = spare[:, nD:nD + nC]
        half_g1 = spare[:, nD + nC:nD + nC + nR]
        wcomb = spare2[:, 0:WIN * nR]
        g02 = spare2[:, WIN * nR:WIN * nR + nR]
        wf_out = xn[:, 2:4].rearrange("p q h r c -> p (q h r c)")[:, 0:nW]
        wf = [wraw, wf_c1, wf_out]
        ws = [wcomb, wf_c1, wf_out]
        w_hi = [wdh[:].rearrange("p w h k m -> p (w h k m)"), wch[:].rearrange("p h m -> p (h m)"),
                wh[:].rearrange("p h k m -> p (h k m)")]
        w_lo = [wdl[:].rearrange("p w h k m -> p (w h k m)"), wcl[:].rearrange("p h m -> p (h m)"),
                wl[:].rearrange("p h k m -> p (h k m)")]

        x_loaded = [sem(f"x_loaded{q}") for q in range(PAIRS)]
        w_loaded = [sem(f"w_loaded{n}") for n in range(3)]
        c_loaded = sem("c_loaded")
        norm_loaded = sem("norm_loaded")
        zeroed = sem("zeroed")
        wmax_done = sem("wmax_done")
        wred_done = sem("wred_done")
        wscale_done = sem("wscale_done")
        whi_done = sem("whi_done")
        wlo_done = sem("wlo_done")
        const_done = sem("const_done")
        chain = sem("chain")
        bn_done = sem("bn_done")
        chan_done = sem("chan_done")
        gmean_done = sem("gmean_done")
        gcopy_done = sem("gcopy_done")
        gdev_done = sem("gdev_done")
        gsq_done = sem("gsq_done")
        gvar_done = sem("gvar_done")
        geps_done = sem("geps_done")
        gpow_done = sem("gpow_done")
        gnewton = sem("gnewton")
        xn_done = sem("xn_done")
        xt_done = sem("xt_done")
        xth_done = sem("xth_done")
        xtl_done = sem("xtl_done")
        xch_done = sem("xch_done")
        xcl_done = sem("xcl_done")
        res_loaded = sem("res_loaded")
        m_done = sem("m_done")
        m12_done = sem("m12_done")
        conv_done = sem("conv_done")
        y_done = sem("y_done")
        d_done = sem("d_done")
        dsb_done = sem("dsb_done")
        dstep = sem("dstep")
        dpart_done = sem("dpart_done")
        s_done = sem("s_done")
        t_done = sem("t_done")
        u_done = sem("u_done")
        hi_done = sem("hi_done")
        lo_done = sem("lo_done")
        used = sem("used")
        drained = sem("drained")
        stored = sem("stored")

        U0, HI0, LO0, USED0, DR0, ST0 = 4, 2, 2, 4, 4, 16

        block = ctx.enter_context(nc.Block())

        def pairs_of(q):
            return (1 if q == 0 else 0), (SR - 1 if q == PAIRS - 1 else SR)

        @block.sync
        def _(sp):
            sp.sem_inc(stored, ST0)
            sp.dma_start(wf[0], w_d1.rearrange("p h k m -> p (h k m)")).then_inc(w_loaded[0], 16)
            sp.dma_start(wf[1], w_c1.rearrange("p h m -> p (h m)")).then_inc(w_loaded[1], 16)

            def load_image(image):
                for q in range(PAIRS):
                    sp.dma_start(xraw[:, :, q * PR * COLS:(q + 1) * PR * COLS],
                                 x_v[image, q]).then_inc(x_loaded[q], 16)

            load_image(0)
            sp.dma_start(ws0[:], w_s0).then_inc(c_loaded, 16)
            sp.dma_start(wd2[:], w_d2).then_inc(c_loaded, 16)
            sp.dma_start(dsel16, delta.rearrange("p b k c -> p (b k c)")).then_inc(c_loaded, 16)
            sp.dma_start(rmix[:], row_mix).then_inc(c_loaded, 16)
            sp.dma_start(wf[2], w_out.rearrange("p h k m -> p (h k m)")).then_inc(w_loaded[2], 16)
            sp.dma_start(osb[:], x_v[0, 0]).then_inc(res_loaded, 16)

            def image(i, last):
                if not last:
                    sp.wait_ge(xn_done, PAIRS * i + PAIRS)
                    load_image(i + 1)
                for q in range(PAIRS):
                    sp.wait_ge(drained, 4 * (PAIRS * i + q) + 4 + DR0)
                    sp.dma_start(out_v[i, q], osb[:]).then_inc(stored, 16)
                    if not (last and q == PAIRS - 1):
                        sp.wait_ge(stored, 16 * (PAIRS * i + q + 1) + ST0)
                        sp.dma_start(osb[:], x_v[i, q + 1] if q < PAIRS - 1 else
                                     x_v[i + 1, 0]).then_inc(res_loaded, 16)

            with sp.Fori(0, B - 1) as i:
                image(i, False)
            image(B - 1, True)
            sp.wait_ge(stored, 16 * B * PAIRS + ST0)

        def row_window(eng, q, c):
            first, second, op = ((0, 2, ALU.subtract), (1, 2, ALU.add), (2, 1, ALU.subtract),
                                 (3, 1, ALU.subtract))[WINDOWS[c]]
            return eng.tensor_tensor(xt[:, c % XT_SLOTS], xn[:, q, :, first:first + 2 * BR - 1:2, :],
                                     xn[:, q, :, second:second + 2 * BR - 1:2, :], op).then_inc(xt_done, 1)

        def row_window_low(eng, q, c):
            def flat(a):
                return a.rearrange("p h r c -> p (h r c)")
            w = WINDOWS[c]
            return eng.tensor_tensor(flat(xtl[:, q % 2, w]), flat(xt[:, c % XT_SLOTS]),
                                     flat(xth[:, q % 2, w]), ALU.subtract).then_inc(xtl_done, 1)

        def inside(q):
            return xn[:, q, :, 1:1 + PR, 1:1 + COLS]

        @block.gpsimd
        def _(pool):
            nc.gpsimd.memset(ghalf[:], -0.5)
            nc.gpsimd.memset(xn[:, 0:2], 0.0).then_inc(zeroed, 1)

            def tensor_max(n):
                pool.wait_ge(wmax_done, n + 1)
                nc.gpsimd.partition_all_reduce(wmaxall[:, n:n + 1], wmax[:, n:n + 1], P,
                                               bass.bass_isa.ReduceOp.max).then_inc(wred_done, 1)

            def root(image):
                pool.wait_ge(geps_done, image + 1)
                nc.gpsimd.tensor_tensor(grs[:], gvar[:], ghalf[:], ALU.pow).then_inc(gpow_done, 1)

            def split_rows(p, q):
                pool.wait_ge(xn_done, p + 1)

                def low_part(c):
                    pool.wait_ge(xt_done, WIN * p + c + 1)
                    pool.wait_ge(xth_done, WIN * p + c + 1)
                    row_window_low(nc.gpsimd, q, c)

                for c in range(WIN):
                    if c < XT_SLOTS:
                        pool.wait_ge(xtl_done, WIN * p)
                    else:
                        low_part(c - XT_SLOTS)
                        pool.wait_ge(xtl_done, WIN * p + c - XT_SLOTS + 1)
                    row_window(nc.gpsimd, q, c)
                for c in range(WIN - XT_SLOTS, WIN):
                    low_part(c)

            def split_inside(p, q):
                pool.wait_ge(xch_done, p + 1)
                nc.gpsimd.tensor_tensor(xcl[:], inside(q), xch[:], ALU.subtract).then_inc(xcl_done, 1)

            tensor_max(0)
            tensor_max(1)
            root(0)
            tensor_max(2)
            split_rows(1, 1)
            pool.wait_ge(wlo_done, 3)
            nc.gpsimd.memset(xn[:, 2:4], 0.0).then_inc(zeroed, 1)
            split_inside(1, 1)

            with pool.Fori(0, B - 1) as i:
                split_rows(PAIRS * i + 2, 2)
                split_inside(PAIRS * i + 2, 2)
                split_rows(PAIRS * i + 3, 3)
                split_inside(PAIRS * i + 3, 3)
                root(i + 1)
                split_rows(PAIRS * i + 4, 0)
                split_inside(PAIRS * i + 4, 0)
                split_rows(PAIRS * i + 5, 1)
                split_inside(PAIRS * i + 5, 1)
            split_rows(PAIRS * (B - 1) + 2, 2)
            split_inside(PAIRS * (B - 1) + 2, 2)
            split_rows(PAIRS * (B - 1) + 3, 3)
            split_inside(PAIRS * (B - 1) + 3, 3)

        @block.scalar
        def _(act):
            act.dma_start(vec[:], vecs).then_inc(norm_loaded, 16)
            act.dma_start(gavg[:], group_avg).then_inc(norm_loaded, 16)

            def weights_high(n):
                act.wait_ge(w_loaded[n], 16)
                act.wait_ge(wscale_done, n + 1)
                nc.scalar.activation(w_hi[n], ws[n], ACT.Copy, scale=wscale[:, n:n + 1]).then_inc(whi_done, 1)

            def tanh(g, l):
                for h in range(H):
                    act.wait_ge(s_done, 2 * g + h + 1)
                    act.wait_ge(u_done, 2 * (g - 2) + h + 1 + U0)
                    nc.scalar.activation(t[:, l % 2, h, :], sc[:, h, :], ACT.Tanh,
                                         bias=tbias[:, h:h + 1]).then_inc(t_done, 1)

            def high(g, l):
                act.wait_ge(u_done, 2 * g + 2 + U0)
                act.wait_ge(used, g - 3 + USED0)
                nc.scalar.activation(uh[:, l % 4, :, :], u[:, l % 2, :, :], ACT.Copy).then_inc(hi_done, 1)

            def rows_high(p, q, c):
                act.wait_ge(xt_done, WIN * p + c + 1)
                nc.scalar.activation(xth[:, q % 2, WINDOWS[c]].rearrange("p h r c -> p (h r c)"),
                                     xt[:, c % XT_SLOTS].rearrange("p h r c -> p (h r c)"),
                                     ACT.Copy).then_inc(xth_done, 1)

            def x_high(p, q):
                act.wait_ge(xn_done, p + 1)
                nc.scalar.activation(xch[:], inside(q), ACT.Copy).then_inc(xch_done, 1)

            def keep_m12(p):
                act.wait_ge(m_done, p + 1)
                nc.scalar.activation(m12[:], yp[:, 1, :], ACT.Copy).then_inc(m12_done, 1)

            def hidden(p):
                act.wait_ge(conv_done, p + 1)
                for b in range(2):
                    for half in range(2):
                        rows = slice(M * half, M * half + M)
                        ins = nc.scalar.activation(y[rows, b, :], yp[rows, 0 if half == b else 1, :], ACT.Relu,
                                                   bias=vec[rows, b:b + 1], scale=yscale[rows, b:b + 1])
                ins.then_inc(y_done, 1)

            def tap_bias(p):
                act.wait_ge(d_done, p + 1)
                nc.scalar.activation(dsb[:], yp[:, 0, :], ACT.Identity, bias=vec[:, 4:5]).then_inc(dsb_done, 1)

            weights_high(0)
            weights_high(1)
            for c in range(WIN):
                rows_high(0, 0, c)
            x_high(0, 0)
            weights_high(2)
            act.wait_ge(norm_loaded, 2 * 16)
            act.wait_ge(const_done, 1)
            keep_m12(0)
            rows_high(1, 1, 0)
            rows_high(1, 1, 1)
            hidden(0)
            rows_high(1, 1, 2)
            tap_bias(0)

            def step(i, l, last):
                q, e = divmod(l, STEPS)
                g, p = IMG * i + l, PAIRS * i + q
                tanh(g, l)
                if not (isinstance(g, int) and g == 0):
                    high(g - 1, (l - 1) % IMG)
                if isinstance(p, int) and p == 0 and e == 1:
                    rows_high(1, 1, 3)
                if isinstance(p, int) and p == 0 and e == 2:
                    x_high(1, 1)
                if not (last and q >= PAIRS - 2):
                    if e in ROWS_HIGH_AT:
                        rows_high(p + 2, (q + 2) % PAIRS, ROWS_HIGH_AT.index(e))
                    if e == X_HIGH_AT:
                        x_high(p + 2, (q + 2) % PAIRS)
                if e == M12_AT and not (last and q == PAIRS - 1):
                    keep_m12(p + 1)
                if e == HIDDEN_AT and not (last and q == PAIRS - 1):
                    hidden(p + 1)
                if e == TAP_BIAS_AT and not (last and q == PAIRS - 1):
                    tap_bias(p + 1)

            for l in range(ROLL):
                step(0, l, False)
            with act.Fori(0, B - 1) as i:
                for l in range(ROLL, IMG):
                    step(i, l, False)
                for l in range(ROLL):
                    step(i + 1, l, False)
            for l in range(ROLL, IMG):
                step(B - 1, l, True)
            high(B * IMG - 1, IMG - 1)

        @block.vector
        def _(dve):
            for s, n in ((u_done, U0), (hi_done, HI0), (lo_done, LO0), (drained, DR0)):
                dve.sem_inc(s, n)
            links = [0]

            def link(ins):
                links[0] += 1
                ins.then_inc(chain, 1)
                dve.wait_ge(chain, links[0])

            def weight_max(n):
                dve.wait_ge(w_loaded[n], 16)
                nc.vector.tensor_reduce(wmax[:, n:n + 1], wf[n], AX.X, ALU.max,
                                        apply_absolute_value=True).then_inc(wmax_done, 1)

            def weight_scale(n):
                dve.wait_ge(wred_done, n + 1)
                c = slice(n, n + 1)
                link(nc.vector.tensor_scalar(wtmp[:, c], wmaxall[:, c], W_TINY, None, ALU.max))
                link(nc.vector.tensor_scalar(wexp[:, c].bitcast(I32), wtmp[:, c].bitcast(I32), 0x7F800000, None,
                                             ALU.bitwise_and))
                link(nc.vector.tensor_scalar(wtmp[:, c], wexp[:, c], 1.0 / W_TOP, None, ALU.mult))
                link(nc.vector.tensor_scalar(wdescale[:, c], wexp[:, c], 1.0 / (W_TOP * X_SCALE), None, ALU.mult))
                nc.vector.reciprocal(wscale[:, c], wtmp[:, c]).then_inc(wscale_done, 1)

            def combine_rows():
                g = wraw.rearrange("p (h y k) -> p y h k", h=H, y=3)
                def part(a):
                    return a.rearrange("p (h k) -> p h k", h=H)
                out = [part(wcomb[:, nR * c:nR * (c + 1)]) for c in range(WIN)]
                nc.vector.tensor_copy(out[0], g[:, 0])
                nc.vector.tensor_copy(out[3], g[:, 2])
                nc.vector.tensor_scalar(part(half_g1), g[:, 1], 0.5, None, ALU.mult)
                link(nc.vector.tensor_tensor(part(g02), g[:, 0], g[:, 2], ALU.add))
                for c, op in ((1, ALU.add), (2, ALU.subtract)):
                    ins = nc.vector.scalar_tensor_tensor(out=out[c], in0=part(g02), scalar=0.5, in1=part(half_g1),
                                                         op0=ALU.mult, op1=op)
                link(ins)

            def weights_low(n):
                dve.wait_ge(whi_done, n + 1)
                dve.wait_ge(wscale_done, n + 1)
                nc.vector.scalar_tensor_tensor(out=w_lo[n], in0=ws[n], scalar=wscale[:, n:n + 1], in1=w_hi[n],
                                               op0=ALU.mult, op1=ALU.subtract).then_inc(wlo_done, 1)

            def stats(image, c):
                q, r = divmod(c, CHUNKS // PAIRS)
                h, k = divmod(r, CHUNKS // PAIRS // H)
                n = q * (CHUNKS // PAIRS // H) + k
                if r == 0:
                    dve.wait_ge(x_loaded[q], 16 * image + 16)
                ins = nc.vector.bn_stats(bnst[:, h, n, :], xraw[:, h, 512 * n:512 * n + 512])
                if c == CHUNKS - 1:
                    ins.then_inc(bn_done, 1)

            def chan_stats(image):
                for h in range(H):
                    ins = nc.vector.bn_aggr(chan[:, h, :], bnst[:, h].rearrange("p n s -> p (n s)"))
                ins.then_inc(chan_done, 1)

            def group_dev(image):
                dve.wait_ge(gmean_done, image + 1)
                nc.vector.tensor_copy(gmean[:], acc[:, 0, 0, 0:H]).then_inc(gcopy_done, 1)
                dve.wait_ge(gcopy_done, image + 1)
                nc.vector.tensor_tensor(gdev[:], chan[:, :, 0], gmean[:], ALU.subtract).then_inc(gdev_done, 1)
                dve.wait_ge(gdev_done, 2 * image + 1)
                nc.vector.tensor_tensor(gdev2[:], gdev[:], gdev[:], ALU.mult).then_inc(gdev_done, 1)
                dve.wait_ge(gdev_done, 2 * image + 2)
                nc.vector.tensor_tensor(gsq[:], gdev2[:], chan[:, :, 1], ALU.add).then_inc(gsq_done, 1)

            def group_eps(image):
                dve.wait_ge(gvar_done, image + 1)
                nc.vector.tensor_scalar(gvar[:], acc[:, 0, 0, 0:H], EPS, None, ALU.add).then_inc(geps_done, 1)

            def group_root(image):
                dve.wait_ge(gpow_done, image + 1)
                nc.vector.tensor_tensor(gn1[:], grs[:], grs[:], ALU.mult).then_inc(gnewton, 1)
                dve.wait_ge(gnewton, 4 * image + 1)
                nc.vector.tensor_tensor(gn2[:], gn1[:], gvar[:], ALU.mult).then_inc(gnewton, 1)
                dve.wait_ge(gnewton, 4 * image + 2)
                nc.vector.tensor_scalar(gn3[:], gn2[:], -0.5 * X_SCALE, 1.5 * X_SCALE, ALU.mult,
                                        ALU.add).then_inc(gnewton, 1)
                dve.wait_ge(gnewton, 4 * image + 3)
                nc.vector.tensor_tensor(rstd[:], grs[:], gn3[:], ALU.mult).then_inc(gnewton, 1)

            def normalise(image, p, q):
                dve.wait_ge(gnewton, 4 * image + 4)
                r0, r1 = pairs_of(q)
                for h in range(H):
                    src = xraw[:, h, (q * PR - 1 + r0) * COLS:(q * PR - 1 + r1) * COLS]
                    ins = nc.vector.tensor_scalar(xn[:, q, h, r0:r1, 1:1 + COLS],
                                                  src.rearrange("p (r c) -> p r c", c=COLS),
                                                  gmean[:, h:h + 1], rstd[:, h:h + 1], ALU.subtract, ALU.mult)
                ins.then_inc(xn_done, 1)

            def split_taps(p, q):
                dve.wait_ge(dsb_done, p + 1)
                nc.vector.tensor_copy(dhi[:, 0], dsb[:]).then_inc(dstep, 1)
                dve.wait_ge(dstep, 3 * p + 1)
                nc.vector.scalar_tensor_tensor(out=dsb[:], in0=dhi[:, 0], scalar=vec[:, 6:7], in1=dsb[:],
                                               op0=ALU.mult, op1=ALU.add).then_inc(dstep, 1)

            def split_taps_2(p, q):
                dve.wait_ge(dstep, 3 * p + 2)
                nc.vector.tensor_copy(dhi[:, 1], dsb[:]).then_inc(dstep, 1)
                dve.wait_ge(dstep, 3 * p + 3)
                nc.vector.scalar_tensor_tensor(out=dpart[:, q % 2], in0=dhi[:, 1], scalar=vec[:, 7:8], in1=dsb[:],
                                               op0=ALU.mult, op1=ALU.add).then_inc(dpart_done, 1)

            def gate(g, l):
                q, e = divmod(l, STEPS)
                b, k = divmod(e, TAPS)
                dy, dx = divmod(k, 3)
                dve.wait_ge(hi_done, g - 1 + HI0)
                dve.wait_ge(lo_done, g - 1 + LO0)
                for h in range(H):
                    dve.wait_ge(t_done, 2 * g + h + 1)
                    nc.vector.scalar_tensor_tensor(
                        out=u[:, l % 2, h, :].rearrange("p (r c) -> p r c", c=COLS),
                        in0=t[:, l % 2, h, :].rearrange("p (r c) -> p r c", c=COLS), scalar=1.0,
                        in1=xn[:, q, h, b + dy:b + dy + PR - 1:2, dx:dx + COLS],
                        op0=ALU.add, op1=ALU.mult).then_inc(u_done, 1)

            def low(g, l):
                dve.wait_ge(hi_done, g + 1 + HI0)
                nc.vector.tensor_tensor(ul[:, l % 4, :, :], u[:, l % 2, :, :], uh[:, l % 4, :, :],
                                        ALU.subtract).then_inc(lo_done, 1)

            def drain(p, b):
                dve.wait_ge(used, TAPS * (2 * p + b + 1) + USED0)
                dve.wait_ge(res_loaded, 16 * p + 16)
                for m in range(H):
                    rows = osb[:, m].rearrange("p (j b c) -> p b j c", b=2, c=COLS)[:, b]
                    nc.vector.scalar_tensor_tensor(
                        out=rows, in0=acc[:, b, m, :].rearrange("p (r c) -> p r c", c=COLS),
                        scalar=wdescale[:, 2:3], in1=rows, op0=ALU.mult, op1=ALU.add).then_inc(drained, 1)

            weight_max(0)
            weight_max(1)
            combine_rows()
            weight_scale(0)
            weight_scale(1)
            for c in range(CHUNKS):
                stats(0, c)
                if c == CHUNKS // PAIRS:
                    weights_low(0)
                    weights_low(1)
            dve.wait_ge(bn_done, 1)
            chan_stats(0)
            group_dev(0)
            group_eps(0)
            group_root(0)
            dve.wait_ge(zeroed, 1)
            normalise(0, 0, 0)
            dve.wait_ge(xn_done, 1)
            for c in range(XT_SLOTS):
                row_window(nc.vector, 0, c)
            for c in range(WIN):
                dve.wait_ge(xt_done, c + 1)
                dve.wait_ge(xth_done, c + 1)
                row_window_low(nc.vector, 0, c)
                if c == 1:
                    dve.wait_ge(xtl_done, 1)
                    row_window(nc.vector, 0, XT_SLOTS)
            weight_max(2)
            normalise(0, 1, 1)
            weight_scale(2)
            dve.wait_ge(xch_done, 1)
            nc.vector.tensor_tensor(xcl[:], inside(0), xch[:], ALU.subtract).then_inc(xcl_done, 1)
            dve.wait_ge(norm_loaded, 2 * 16)
            dve.wait_ge(c_loaded, 4 * 16)
            for b in range(2):
                for half, n in ((b, 0), (1 - b, 1)):
                    rows = slice(M * half, M * half + M)
                    nc.vector.tensor_copy(yscale[rows, b:b + 1], wdescale[rows, n:n + 1])
            for h in range(H):
                nc.vector.tensor_tensor(tbias[:, h:h + 1], vec[:, 2 + h:3 + h], vec[:, 5:6], ALU.add)
            nc.vector.tensor_copy(dsel[:].rearrange("p b k c -> p (b k c)"), dsel16).then_inc(const_done, 1)
            weights_low(2)
            split_taps(0, 0)
            split_taps_2(0, 0)

            def step(i, l, last):
                q, e = divmod(l, STEPS)
                g, p = IMG * i + l, PAIRS * i + q
                if e == 0:
                    dve.wait_ge(xn_done, p + 1)
                if q == 1 and e == STATS_AT + CHUNKS // 2 and not last:
                    dve.wait_ge(bn_done, i + 2)
                gate(g, l)
                if not (isinstance(g, int) and g == 0):
                    low(g - 1, (l - 1) % IMG)
                start = isinstance(p, int) and p == 0
                if e == (4 if start else 1) and q < 2:
                    if start:
                        dve.wait_ge(zeroed, 2)
                    normalise(i, p + 2, q + 2)
                if e == 4 and q >= 2 and not last:
                    normalise(i + 1, p + 2, q - 2)
                if e == DRAIN_AT and not (isinstance(p, int) and p == 0):
                    drain(p - 1, 1)
                if e == TAPS + DRAIN_AT:
                    drain(p, 0)
                if e == SPLIT_TAPS_AT and not (last and q == PAIRS - 1):
                    split_taps(p + 1, q + 1)
                if e == SPLIT_TAPS_AT + 1 and not (last and q == PAIRS - 1):
                    split_taps_2(p + 1, q + 1)
                if not last:
                    if q == 1 and STATS_AT <= e < STATS_AT + CHUNKS // 2:
                        stats(i + 1, 2 * (e - STATS_AT))
                        stats(i + 1, 2 * (e - STATS_AT) + 1)
                    if q == 1 and e == STATS_AT + CHUNKS // 2:
                        chan_stats(i + 1)
                    if q == 2 and e == 0:
                        group_dev(i + 1)
                    if q == 2 and e == 2:
                        group_eps(i + 1)
                    if q == 2 and e == 3:
                        group_root(i + 1)

            for l in range(ROLL):
                step(0, l, False)
            with dve.Fori(0, B - 1) as i:
                for l in range(ROLL, IMG):
                    step(i, l, False)
                for l in range(ROLL):
                    step(i + 1, l, False)
            for l in range(ROLL, IMG):
                step(B - 1, l, True)
            low(B * IMG - 1, IMG - 1)
            drain(PAIRS * B - 1, 1)

        @block.tensor
        def _(pe):
            pe.sem_inc(used, USED0)

            def scores(g, l, p):
                q, e = divmod(l, STEPS)
                b, k = divmod(e, TAPS)
                if k == 0 and b == 0:
                    pe.wait_ge(y_done, p + 1)
                if k == 1 and b == 0:
                    pe.wait_ge(dpart_done, p + 1)
                for h in range(H):
                    if not (isinstance(g, int) and g == 0):
                        pe.wait_ge(t_done, 2 * (g - 1) + h + 1)
                    if k == 0:
                        ins = nc.tensor.matmul(sc[:, h, :], ws0[:, b, h * P:(h + 1) * P], y[:, b, :],
                                               start=True, stop=True)
                    else:
                        ins = nc.tensor.matmul(sc[:, h, :], dsel[:, b, k - 1, :], dpart[:, q % 2, :],
                                               start=False, stop=True, skip_group_check=True)
                    ins.then_inc(s_done, 1)

            def outputs(g, l, n):
                b, k = divmod(l % STEPS, TAPS)
                pe.wait_ge(lo_done, g + 1 + LO0)
                if k == 0:
                    pe.wait_ge(drained, 2 * (n - 1) + DR0)
                for h in range(H):
                    for m in range(H):
                        cols = slice(m * P, (m + 1) * P)
                        for j, (w, v) in enumerate(((wh, uh), (wh, ul), (wl, uh))):
                            ins = nc.tensor.matmul(acc[:, b, m, :], w[:, h, k, cols], v[:, l % 4, h, :],
                                                   start=(k == 0 and h == 0 and j == 0),
                                                   stop=(k == TAPS - 1 and h == H - 1 and j == 2))
                ins.then_inc(used, 1)

            slots = [(pair, h, k, j) for pair in ((0, 3), (1, 2)) for h in range(H) for k in range(3)
                     for j in range(3)]

            def conv_slots(p, q, first, count):
                for s in range(first, min(first + count, len(slots))):
                    pair, h, k, j = slots[s]
                    if s in (0, len(slots) // 2):
                        pe.wait_ge(xtl_done, WIN * p + (2 if s == 0 else WIN))
                    for half, c in enumerate(pair):
                        ins = nc.tensor.matmul(
                            yp[M * half:M * half + M, 0 if pair[0] == 0 else 1, :],
                            (wdh, wdh, wdl)[j][:, c, h, k, :],
                            (xth, xtl, xth)[j][:, q % 2, c, h, :, k:k + COLS],
                            start=(h == 0 and k == 0 and j == 0), stop=(h == H - 1 and k == 2 and j == 2))
                    if s == len(slots) - 1:
                        ins.then_inc(m_done, 1)

            def row_sums(p):
                pe.wait_ge(m12_done, p + 1)
                nc.tensor.matmul(yp[:, 0, :], rmix[:], m12[:], start=False, stop=True, skip_group_check=True)

            def channel_slots(p, h):
                if h == 0:
                    pe.wait_ge(xcl_done, p + 1)
                for j in range(3):
                    for half in range(2):
                        ins = nc.tensor.matmul(
                            yp[M * half:M * half + M, 1, :], (wch, wch, wcl)[j][:, h, :],
                            (xch, xcl, xch)[j][:, h, 1 - half:PR:2, :],
                            start=(h == 0 and j == 0), stop=(h == H - 1 and j == 2))
                if h == H - 1:
                    ins.then_inc(conv_done, 1)

            def tap_products(p):
                pe.wait_ge(y_done, p + 1)
                for b in range(2):
                    ins = nc.tensor.matmul(yp[M * b:M * b + M, 0, :], wd2[:, b, :], y[:, b, :], start=True, stop=True)
                ins.then_inc(d_done, 1)

            def group_mean(image):
                pe.wait_ge(chan_done, image + 1)
                nc.tensor.matmul(acc[:, 0, 0, 0:H], gavg[:], chan[:, :, 0], start=True,
                                 stop=True).then_inc(gmean_done, 1)

            def group_var(image):
                pe.wait_ge(gsq_done, image + 1)
                nc.tensor.matmul(acc[:, 0, 0, 0:H], gavg[:], gsq[:], start=True, stop=True).then_inc(gvar_done, 1)

            pe.wait_ge(norm_loaded, 2 * 16)
            group_mean(0)
            group_var(0)
            pe.wait_ge(wlo_done, 2)
            conv_slots(0, 0, 0, len(slots))
            pe.wait_ge(c_loaded, 4 * 16)
            row_sums(0)
            channel_slots(0, 0)
            channel_slots(0, 1)
            tap_products(0)
            pe.wait_ge(const_done, 1)
            for g in range(LEAD):
                scores(g, g, 0)
            pe.wait_ge(wlo_done, 3)

            def image(i, last):
                for q in range(PAIRS):
                    final = last and q == PAIRS - 1
                    for e in range(STEPS):
                        l = q * STEPS + e
                        g, p = IMG * i + l, PAIRS * i + q
                        la = (l + LEAD) % IMG
                        if not (last and l + LEAD >= IMG):
                            scores(g + LEAD, la, p + (1 if e + LEAD >= STEPS else 0))
                        if q == 2 and e == 0 and not last:
                            pe.wait_ge(geps_done, i + 2)
                        outputs(g, l, 2 * p + e // TAPS)
                        if not final:
                            if e == 0:
                                pe.wait_ge(dsb_done, p + 1)
                            conv_slots(p + 1, (q + 1) % PAIRS, e * CONV_SLOTS, CONV_SLOTS)
                            if e == ROW_SUMS_AT:
                                row_sums(p + 1)
                            if e in (ROW_SUMS_AT, ROW_SUMS_AT + 1):
                                channel_slots(p + 1, e - ROW_SUMS_AT)
                            if e == TAP_PRODUCTS_AT:
                                tap_products(p + 1)
                        if q == 1 and not last:
                            if e == 14:
                                pe.wait_ge(drained, 4 * p + 2 + DR0)
                                group_mean(i + 1)
                            if e == 16:
                                group_var(i + 1)

            with pe.Fori(0, B - 1) as i:
                image(i, False)
            image(B - 1, True)


_OUT_SHAPE = (8, 256, 64, 64)


def kernel(**inputs):
    import numpy as np
    import concourse.bacc as _bacc
    from concourse import mybir as _mybir
    from concourse.bass_utils import run_bass_kernel_spmd as _run

    a = {k.replace("L0_conv_", ""): np.asarray(v) for k, v in inputs.items()}
    x = a["x"]
    H, M, C = 2, a["w_c1"].shape[0], x.shape[1]
    w_d1 = a["w_d1"].reshape(M, H, P, TAPS).transpose(2, 1, 3, 0)
    w_c1 = a["w_c1"].reshape(M, H, P).transpose(2, 1, 0)
    w_out = a["W"].reshape(C, H, P, TAPS).transpose(2, 1, 3, 0)
    tap0 = np.broadcast_to(a["w_d2"][0][:, None], (M, C))
    w_s0 = np.stack([np.concatenate([tap0, a["w_c2"].T]), np.concatenate([a["w_c2"].T, tap0])], 1)
    w_d2 = np.zeros((P, 2, M), np.float32)
    vecs = np.zeros((P, 8), np.float32)
    delta = np.zeros((P, 2, TAPS - 1, P), np.float16)
    for b in range(2):
        for c in range(D_COPIES):
            r = M * b + TAPS * c
            w_d2[M * b:M * b + M, b, TAPS * c:TAPS * c + TAPS] = a["w_d2"].T
            vecs[r:r + TAPS, 4] = a["b_d2"]
            vecs[r:r + TAPS, 6] = -1.0 if c >= 1 else 0.0
            vecs[r:r + TAPS, 7] = -1.0 if c >= 2 else 0.0
            for k in range(TAPS - 1):
                delta[r + k + 1, b, k] = 1
                delta[r + k, b, k] = -1
    vecs[:, 0] = np.concatenate([a["b_d1"], a["b_c1"]])
    vecs[:, 1] = np.concatenate([a["b_c1"], a["b_d1"]])
    vecs[:, 2] = a["b_c2"][0:P]
    vecs[:, 3] = a["b_c2"][P:2 * P]
    vecs[:, 5] = a["b_d2"][0]
    group_avg = np.kron(np.eye(P // GROUP, dtype=np.float32), np.full((GROUP, GROUP), 1.0 / GROUP, np.float32))

    row_mix = np.kron(np.array([[1, 1], [1, -1]], np.float32), np.eye(M, dtype=np.float32))

    nc = _bacc.Bacc("TRN2", target_bir_lowering=False, num_devices=1)
    arrays, args = {}, []
    for name, v in (("x", x), ("w_d1", w_d1), ("w_c1", w_c1), ("w_out", w_out), ("w_s0", w_s0), ("w_d2", w_d2),
                    ("vecs", vecs), ("delta", delta), ("group_avg", group_avg),
                    ("row_mix", row_mix)):
        v = np.ascontiguousarray(v)
        arrays[f"in_{name}_dram"] = v
        args.append(nc.dram_tensor(f"in_{name}_dram", v.shape, _mybir.dt.from_np(v.dtype), kind="ExternalInput").ap())
    args.append(nc.dram_tensor("out_0_dram", _OUT_SHAPE, _mybir.dt.float32, kind="ExternalOutput").ap())
    build(nc, *args)
    r = _run(nc, [arrays], core_ids=[0])
    return r.results[0]["out_0_dram"]
```
